# Optimizing a Trainium2 kernel written in Bass

```python
import numpy as np
import jax
import jax.numpy as jnp

def _softmax(x, axis=-1):
    return jax.nn.softmax(x, axis=axis)

def _gelu(x):
    return jax.nn.gelu(x, approximate=True)

def _silu(x):
    return jax.nn.silu(x)

def _sigmoid(x):
    return jax.nn.sigmoid(x)

def _layernorm(x, axis=-1, eps=1e-05):
    m = jnp.mean(x, axis=axis, keepdims=True)
    v = jnp.var(x, axis=axis, keepdims=True)
    return (x - m) / jnp.sqrt(v + eps)

def _scatter_add(tgt, idx, src, axis=0):
    return tgt.at[idx].add(src)

def _segment_sum(src, seg, n):
    return jax.ops.segment_sum(src, seg, n)
kernel_name = 'mk_adj_preln_d2_adj_r2_7ee320'

def setup_inputs(seed: int=0):
    np.random.seed(seed)
    _w = jnp.asarray

    def _rec_inputs():
        import jax
        import jax.numpy as jnp
        _gk = jax.random.key(seed)
        x = -0.0005207 + 1.001 * jax.random.normal(jax.random.fold_in(_gk, 1), (8192, 128), jnp.float32)
        _a = jax.random.bernoulli(jax.random.fold_in(_gk, 2), 0.00195312, (8192, 8192))
        _a = jnp.logical_or(_a, jnp.swapaxes(_a, -1, -2))
        _a = jnp.logical_or(_a, jnp.eye(8192, dtype=bool))
        _af = _a.astype(jnp.float32)
        _af = _af * jax.random.uniform(jax.random.fold_in(_gk, 3), (8192, 8192), jnp.float32, 0.05, 1)
        adj = _af
        return (x, adj)
    x, adj = _rec_inputs()

    def _L0_gnn_setup():
        import jax, jax.numpy as jnp
        import numpy as np
        N = 4096
        F_IN = 128
        F_OUT = 128
        key = jax.random.key(seed)
        k1, k2, k3, k4 = jax.random.split(key, 4)
        x = jax.random.normal(k1, (N, F_IN), dtype=jnp.float32)
        adj = jax.random.uniform(k2, (N, N), dtype=jnp.float32)
        bound = 1.0 / np.sqrt(F_IN)
        W = jax.random.uniform(k3, (F_OUT, F_IN), dtype=jnp.float32, minval=-bound, maxval=bound)
        b = jax.random.uniform(k4, (F_OUT,), dtype=jnp.float32, minval=-bound, maxval=bound)
        return {'x': x, 'adj': adj, 'W': W, 'b': b}
    _L0_gnn_all = _L0_gnn_setup()
    _L0_gnn_in = {k: v for k, v in _L0_gnn_all.items() if k in ('W', 'b')}
    del _L0_gnn_all

    def _L1_gnn_setup():
        import jax, jax.numpy as jnp
        import numpy as np
        from jax import lax
        D_MODEL = 128
        D_STATE = 16
        D_CONV = 4
        EXPAND = 2
        D_INNER = EXPAND * D_MODEL
        DT_RANK = (D_MODEL + 15) // 16
        N = 2048
        EPS = 1e-05

        def _mamba(h, w_in, conv_w, conv_b, w_xp, w_dt, b_dt, A_log, D_skip, w_out):
            L = h.shape[0]
            xz = h @ w_in
            xc, z = (xz[:, :D_INNER], xz[:, D_INNER:])
            xpad = jnp.pad(xc, ((D_CONV - 1, 0), (0, 0)))
            xconv = sum((xpad[k:k + L] * conv_w[:, k] for k in range(D_CONV))) + conv_b
            u = jax.nn.silu(xconv)
            dbc = u @ w_xp
            dt = jax.nn.softplus(dbc[:, :DT_RANK] @ w_dt + b_dt)
            B = dbc[:, DT_RANK:DT_RANK + D_STATE]
            C = dbc[:, DT_RANK + D_STATE:]
            A = -jnp.exp(A_log)
            dA = jnp.exp(dt[:, :, None] * A[None])
            dBu = dt[:, :, None] * B[:, None, :] * u[:, :, None]

            def step(hst, inp):
                dAt, dBut, Ct = inp
                hst = dAt * hst + dBut
                return (hst, hst @ Ct)
            _, ys = lax.scan(step, jnp.zeros((D_INNER, D_STATE), h.dtype), (dA, dBu, C))
            y = ys + u * D_skip
            y = y * jax.nn.silu(z)
            return y @ w_out
        key = jax.random.key(seed)
        ks = jax.random.split(key, 16)
        x = jax.random.normal(ks[0], (N, D_MODEL), dtype=jnp.float32)
        a = jax.random.uniform(ks[1], (N, N), dtype=jnp.float32)
        adj = a / a.sum(axis=1, keepdims=True)
        s = lambda fi, fo: 1.0 / np.sqrt(fi)
        gcn_w = jax.random.uniform(ks[2], (D_MODEL, D_MODEL), jnp.float32, -s(D_MODEL, 0), s(D_MODEL, 0))
        gcn_b = jnp.zeros((D_MODEL,), jnp.float32)
        ln_g = jnp.ones((D_MODEL,), jnp.float32)
        ln_b = jnp.zeros((D_MODEL,), jnp.float32)
        w_in = jax.random.normal(ks[3], (D_MODEL, 2 * D_INNER), jnp.float32) * s(D_MODEL, 0)
        conv_w = jax.random.normal(ks[4], (D_INNER, D_CONV), jnp.float32) * s(D_CONV, 0)
        conv_b = jnp.zeros((D_INNER,), jnp.float32)
        w_xp = jax.random.normal(ks[5], (D_INNER, DT_RANK + 2 * D_STATE), jnp.float32) * s(D_INNER, 0)
        w_dt = jax.random.normal(ks[6], (DT_RANK, D_INNER), jnp.float32) * s(DT_RANK, 0)
        b_dt = jnp.log(jnp.expm1(jnp.exp(jax.random.uniform(ks[7], (D_INNER,), jnp.float32, np.log(0.001), np.log(0.1)))))
        A_log = jnp.log(jnp.broadcast_to(jnp.arange(1, D_STATE + 1, dtype=jnp.float32), (D_INNER, D_STATE)))
        D_skip = jnp.ones((D_INNER,), jnp.float32)
        w_out = jax.random.normal(ks[8], (D_INNER, D_MODEL), jnp.float32) * s(D_INNER, 0)
        return dict(x=x, adj=adj, gcn_w=gcn_w, gcn_b=gcn_b, ln_g=ln_g, ln_b=ln_b, w_in=w_in, conv_w=conv_w, conv_b=conv_b, w_xp=w_xp, w_dt=w_dt, b_dt=b_dt, A_log=A_log, D_skip=D_skip, w_out=w_out)
    _L1_gnn_all = _L1_gnn_setup()
    _L1_gnn_in = {k: v for k, v in _L1_gnn_all.items() if k in ('gcn_w', 'gcn_b', 'ln_g', 'ln_b', 'w_in', 'conv_w', 'conv_b', 'w_xp', 'w_dt', 'b_dt', 'A_log', 'D_skip', 'w_out')}
    del _L1_gnn_all
    return {'x': x, 'adj': adj, 'L0_gnn_W': _L0_gnn_in['W'], 'L0_gnn_b': _L0_gnn_in['b'], 'L1_gnn_gcn_w': _L1_gnn_in['gcn_w'], 'L1_gnn_gcn_b': _L1_gnn_in['gcn_b'], 'L1_gnn_ln_g': _L1_gnn_in['ln_g'], 'L1_gnn_ln_b': _L1_gnn_in['ln_b'], 'L1_gnn_w_in': _L1_gnn_in['w_in'], 'L1_gnn_conv_w': _L1_gnn_in['conv_w'], 'L1_gnn_conv_b': _L1_gnn_in['conv_b'], 'L1_gnn_w_xp': _L1_gnn_in['w_xp'], 'L1_gnn_w_dt': _L1_gnn_in['w_dt'], 'L1_gnn_b_dt': _L1_gnn_in['b_dt'], 'L1_gnn_A_log': _L1_gnn_in['A_log'], 'L1_gnn_D_skip': _L1_gnn_in['D_skip'], 'L1_gnn_w_out': _L1_gnn_in['w_out']}

def reference(x, adj, L0_gnn_W, L0_gnn_b, L1_gnn_gcn_w, L1_gnn_gcn_b, L1_gnn_ln_g, L1_gnn_ln_b, L1_gnn_w_in, L1_gnn_conv_w, L1_gnn_conv_b, L1_gnn_w_xp, L1_gnn_w_dt, L1_gnn_b_dt, L1_gnn_A_log, L1_gnn_D_skip, L1_gnn_w_out):
    import jax
    import jax.numpy as jnp

    def _L0_gnn_ref(x, adj, W, b):
        import jax, jax.numpy as jnp
        import numpy as np
        N = 4096
        F_IN = 128
        F_OUT = 128
        D = jnp.sum(adj, axis=1)
        d_inv_sqrt = jnp.power(D + 1e-09, -0.5)
        adj_norm = adj * d_inv_sqrt[:, None] * d_inv_sqrt[None, :]
        h = adj_norm @ x
        out = h @ W.T + b
        return jax.nn.relu(out)

    def _L1_gnn_ref(x, adj, gcn_w, gcn_b, ln_g, ln_b, w_in, conv_w, conv_b, w_xp, w_dt, b_dt, A_log, D_skip, w_out):
        import jax, jax.numpy as jnp
        import numpy as np
        from jax import lax
        D_MODEL = 128
        D_STATE = 16
        D_CONV = 4
        EXPAND = 2
        D_INNER = EXPAND * D_MODEL
        DT_RANK = (D_MODEL + 15) // 16
        N = 2048
        EPS = 1e-05

        def _mamba(h, w_in, conv_w, conv_b, w_xp, w_dt, b_dt, A_log, D_skip, w_out):
            L = h.shape[0]
            xz = h @ w_in
            xc, z = (xz[:, :D_INNER], xz[:, D_INNER:])
            xpad = jnp.pad(xc, ((D_CONV - 1, 0), (0, 0)))
            xconv = sum((xpad[k:k + L] * conv_w[:, k] for k in range(D_CONV))) + conv_b
            u = jax.nn.silu(xconv)
            dbc = u @ w_xp
            dt = jax.nn.softplus(dbc[:, :DT_RANK] @ w_dt + b_dt)
            B = dbc[:, DT_RANK:DT_RANK + D_STATE]
            C = dbc[:, DT_RANK + D_STATE:]
            A = -jnp.exp(A_log)
            dA = jnp.exp(dt[:, :, None] * A[None])
            dBu = dt[:, :, None] * B[:, None, :] * u[:, :, None]

            def step(hst, inp):
                dAt, dBut, Ct = inp
                hst = dAt * hst + dBut
                return (hst, hst @ Ct)
            _, ys = lax.scan(step, jnp.zeros((D_INNER, D_STATE), h.dtype), (dA, dBu, C))
            y = ys + u * D_skip
            y = y * jax.nn.silu(z)
            return y @ w_out
        h = jax.nn.relu(adj @ x @ gcn_w + gcn_b)
        mu = h.mean(-1, keepdims=True)
        var = h.var(-1, keepdims=True)
        h = (h - mu) * lax.rsqrt(var + EPS) * ln_g + ln_b
        return _mamba(h, w_in, conv_w, conv_b, w_xp, w_dt, b_dt, A_log, D_skip, w_out)
    h = jnp.maximum(_layernorm(x, axis=-1), 0.0)
    x = x + _L0_gnn_ref(h, adj, L0_gnn_W, L0_gnn_b)
    h = jnp.maximum(_layernorm(x, axis=-1), 0.0)
    x = x + _L1_gnn_ref(h, adj, L1_gnn_gcn_w, L1_gnn_gcn_b, L1_gnn_ln_g, L1_gnn_ln_b, L1_gnn_w_in, L1_gnn_conv_w, L1_gnn_conv_b, L1_gnn_w_xp, L1_gnn_w_dt, L1_gnn_b_dt, L1_gnn_A_log, L1_gnn_D_skip, L1_gnn_w_out)
    return x

_drawn_inputs = setup_inputs


def setup_inputs(seed=0):
    import zlib

    import numpy as np

    out = dict(_drawn_inputs(seed))
    spreads = {'L1_gnn_gcn_b': (0.0, 0.356),
     'L1_gnn_ln_g': (1.0, 0.2),
     'L1_gnn_ln_b': (0.0, 0.1),
     'L1_gnn_conv_b': (0.0, 0.1),
     'L1_gnn_D_skip': (1.0, 0.2)}
    factors = {'L1_gnn_w_dt': 3.691}
    for name, (base, spread) in spreads.items():
        noise = np.random.default_rng([zlib.crc32(name.encode()), seed]).standard_normal(out[name].shape)
        drawn = base * np.exp(spread * noise) if base else spread * noise
        out[name] = jnp.asarray(drawn.astype(out[name].dtype))
    for name, factor in factors.items():
        out[name] = (out[name] * factor).astype(out[name].dtype)
    return out
```

```python
from contextlib import ExitStack

import concourse.bass as bass
from concourse import mybir

P = 128
N = 8192
F = 128
DI = 256
DS = 16
RANK = 8
HALVES = DI // P
STRIP = 1024
NS = N // STRIP
TPS = STRIP // P
BJ = 512
JT = BJ // P
NB = N // BJ
BPS = STRIP // BJ
BLOCK = JT * STRIP
MM = 512
RING = 4
T = 512
NCH = N // T
CPS = STRIP // T
CT = T // P
NBC = 2 * DS
KP = 3 * NBC
KD = KP + RANK
CONV = 4
LN_EPS = 1e-5
DEG_EPS = 1e-9
HSB = 4

F32 = mybir.dt.float32
BF16 = mybir.dt.bfloat16
ALU = mybir.AluOpType
ACT = mybir.ActivationFunctionType


def pass_a_order(i):
    lower, upper = list(range(BPS * i)), list(range(BPS * (i + 1), NB))
    total, products = len(lower) + len(upper), len(lower)
    return [(lower if (n + 1) * products // total > n * products // total else upper).pop(0) for n in range(total)]


def build(nc, adj, x, w0t, b0, gcn_w, gcn_b, ln_g, ln_b, w_in, conv_w, conv_b, w_x, w_dt, b_dt, a_log, d_skip,
          w_out, ident_in, out):
    x1_dram = nc.dram_tensor("x1_scratch", (P, N // P * F), F32, kind="Internal").ap()
    upper1_dram = nc.dram_tensor("upper1_scratch", (P, N), F32, kind="Internal").ap()

    loads = [("A", i, s) for i in range(NS) for s in pass_a_order(i)]
    loads += [("B", i, s) for i in reversed(range(NS)) for s in reversed(range(BPS * (i + 1), NB))]
    loads += [("C", i, s) for i in range(NS) for s in range(BPS * (i + 1))]
    load_at = {key: q for q, key in enumerate(loads)}

    adds_at, blocks_at = {}, {}
    adds = blocks = 0
    for i in range(NS):
        for n, s in enumerate(pass_a_order(i)):
            adds += n > 0
            adds_at[load_at["A", i, s]] = adds + (n == 0)
            if s < BPS * i:
                blocks += 1
                blocks_at[load_at["A", i, s]] = blocks
        adds += BPS
    adds_per_strip = NB - 1
    assert adds == NS * adds_per_strip
    for q, (phase, _, _) in enumerate(loads):
        if phase != "A":
            blocks += 1
            blocks_at[q] = blocks

    FIRST_SLOT, LAST_SLOT = -DS, NCH * DS + 8
    products = {g: [] for g in range(FIRST_SLOT - 1, LAST_SLOT)}
    for i in range(NS):
        mms = [(i, s, a, h) for s in range(BPS * (i + 1)) for a in range(JT) for h in range(STRIP // MM)]
        if i == 0:
            products[FIRST_SLOT - 1] += mms
            continue
        start, end = DS * (CPS * i - 3) + 4, DS * (CPS * i - 1) + 2
        for n, mm in enumerate(mms):
            products[start + n * (end - start) // len(mms)].append(mm)

    misc = []
    for g in range(FIRST_SLOT, LAST_SLOT):
        k, n = divmod(g, DS)
        if n == 5 and 0 <= k - 1 < NCH:
            misc.append(("out", k - 1))
        if 0 <= k + 1 < NCH:
            misc += {3: [("gcn", k + 1)], 6: [("tr", k + 1)], 7: [("xz0", k + 1)], 8: [("xz1", k + 1)],
                     9: [("xz2", k + 1)], 10: [("xz3", k + 1)], 11: [("dbc", k + 1)],
                     12: [("dt0", k + 1), ("dt1", k + 1)]}.get(n, [])
    misc_at = {key: m for m, key in enumerate(misc)}

    with ExitStack() as ctx:
        def sb(name, shape, dt=F32):
            return ctx.enter_context(nc.sbuf_tensor(name, shape, dt))

        def sem(name):
            return ctx.enter_context(nc.semaphore(name))

        ring = sb("ring", [P, RING, BLOCK])
        diag_h1 = sb("diag_h1", [P, BPS * BLOCK])
        diag = diag_h1[:, :].rearrange("p (b c) -> p b c", b=BPS)
        h1 = diag_h1[:, 0:N]
        arena = sb("arena", [P, 3 * N])
        h0 = arena[:, 0:N]
        part = arena[:, N:2 * N]
        top = [2 * N]

        def work(cols):
            top[0] += cols
            assert top[0] <= 3 * N
            return arena[:, top[0] - cols:top[0]]

        xs = [work(STRIP) for _ in range(2)]
        after_xs = top[0]
        rowacc = work(BLOCK)
        top[0] = after_xs
        s0 = work(STRIP)
        pre = work(STRIP)
        x1 = [work(STRIP) for _ in range(2)]
        l1_stage = work(STRIP)
        top[0] = 0

        def work2(*dims):
            size = 1
            for d in dims:
                size *= d
            v = work(size)
            if len(dims) == 2:
                v = v.rearrange("p (a b) -> p a b", a=dims[0])
            return v

        s1 = work2(STRIP)
        l1_part = s1
        gbuf = work2(CT, F)
        h_t = work2(T)
        xcp = [work2(HALVES, T + CONV) for _ in range(2)]
        cv = work2(HALVES, T)
        u = [work2(HALVES, T) for _ in range(2)]
        sz = [work2(HALVES, T) for _ in range(2)]
        bcv = work2(T)
        dt = [work2(HALVES, T) for _ in range(2)]
        w = [work2(HALVES, T) for _ in range(2)]
        da = [work2(HALVES, T) for _ in range(2)]
        dbu = work2(HALVES, T)
        hs = [work2(HALVES, T) for _ in range(HSB)]
        csb = [work2(T) for _ in range(2)]
        yg = work2(HALVES, T)
        x1t = [work2(CT, F) for _ in range(2)]
        parts = [sb(f"parts{i}", [KP, T], BF16) for i in range(2)]

        ident = sb("ident", [P, P])
        pick = sb("pick", [KP, NBC], BF16)
        ones = sb("ones", [P, 1])
        w0t_sb = sb("w0t_sb", [P, F])
        b0_sb = sb("b0_sb", [P, F])
        gw_sb = sb("gw_sb", [P, F])
        gb_sb = sb("gb_sb", [P, F])
        ln_sb = sb("ln_sb", [P, 2])
        w_in_sb = sb("w_in_sb", [P, 2 * DI])
        conv_sb = sb("conv_sb", [P, HALVES, CONV])
        cols_sb = sb("cols_sb", [P, 3, HALVES])
        wx_sb = sb("wx_sb", [P, HALVES, KD])
        wdt_sb = sb("wdt_sb", [P, DI])
        a_sb = sb("a_sb", [P, HALVES, DS])
        wo_sb = sb("wo_sb", [P, HALVES, F])
        state = sb("state", [P, HALVES, DS])
        dcol = sb("dcol", [P, N // P])
        stats = sb("stats", [P, TPS, 6])
        mv = sb("mv", [P, TPS, 2])
        base = sb("base", [P, TPS])
        minus_half = sb("minus_half", [P, TPS])
        rstd = sb("rstd", [P, TPS])
        nmr = sb("nmr", [P, TPS])

        ps = ctx.enter_context(nc.psum_tensor("ps", [P, 8, MM], F32))
        acc0 = [ps[:, 0:2, :], ps[:, 2:4, :]]
        ps_deg = ps[:, 4, 0:TPS]
        acc1 = ps[:, 4:6, :]
        ps_w = ps[:, 6:8, :]
        acc_c = ps[:, 2:4, :]
        y_ps = ps[:, 0:2, :]
        b_ps = [ps[:, 4, :], ps[:, 5, :]]
        c_ps = ps[:, 6, :]
        m_ps = ps[:, 7, :]

        weights_in = sem("weights_in")
        ring_in = [sem(f"ring_in{i}") for i in range(RING)]
        diag_in = [sem(f"diag_in{i}") for i in range(BPS)]
        xs_in = [sem(f"xs_in{i}") for i in range(2)]
        consts_done = sem("consts_done")
        a_done = sem("a_done")
        dve_step = sem("dve_step")
        adds_done = sem("adds_done")
        blocks_done = sem("blocks_done")
        diag_done = sem("diag_done")
        fold_done = sem("fold_done")
        base_ready = sem("base_ready")
        pow_done = sem("pow_done")
        norm_ready = sem("norm_ready")
        normed = sem("normed")
        h0_ready = sem("h0_ready")
        part_ready = sem("part_ready")
        layer0_sum = sem("layer0_sum")
        s0_ready = sem("s0_ready")
        w_done = sem("w_done")
        x1_ready = sem("x1_ready")
        x1_out = [sem(f"x1_out{i}") for i in range(2)]
        l1_staged = sem("l1_staged")
        l1_out = sem("l1_out")
        l1_back = sem("l1_back")
        s1_ready = sem("s1_ready")
        misc_full = sem("misc_full")
        misc_free = sem("misc_free")
        act_step = sem("act_step")
        conv_done = sem("conv_done")
        u_ready = sem("u_ready")
        sz_ready = sem("sz_ready")
        parts_ready = sem("parts_ready")
        ex_ready = sem("ex_ready")
        w1_ready = sem("w1_ready")
        log_ready = sem("log_ready")
        dt_ready = sem("dt_ready")
        b_ready = sem("b_ready")
        c_ready = sem("c_ready")
        c_copied = sem("c_copied")
        da_ready = sem("da_ready")
        dbu_done = sem("dbu_done")
        scan_done = sem("scan_done")
        state_saved = sem("state_saved")
        mult_done = sem("mult_done")
        pair_done = sem("pair_done")
        nsum_done = sem("nsum_done")
        y_free = sem("y_free")
        yg_ready = sem("yg_ready")
        x1t_in = [sem(f"x1t_in{i}") for i in range(2)]
        o_ready = sem("o_ready")
        out_done = [sem(f"out_done{i}") for i in range(2)]

        NORM_C = 2 * NS

        block = ctx.enter_context(nc.Block())

        def tile_of(h, t):
            return h[:, t * F:(t + 1) * F]

        def rows(v, n):
            return v.rearrange("p (t f) -> p t f", t=n)

        def halves(v):
            return v.rearrange("p (h c) -> p h c", c=MM)

        def evacuated(eng, kind, k):
            eng.wait_ge(misc_free, misc_at[kind, k] + 1)

        weight_loads = [
            (ident[:, :], ident_in), (w0t_sb[:, :], w0t), (b0_sb[:, :], b0.to_broadcast([P, F])),
            (gw_sb[:, :], gcn_w), (gb_sb[:, :], gcn_b.to_broadcast([P, F])),
            (ln_sb[:, 0:1], ln_g), (ln_sb[:, 1:2], ln_b), (w_in_sb[:, :], w_in),
            (conv_sb[:, :, :], conv_w), (cols_sb[:, 0, :], conv_b), (cols_sb[:, 1, :], b_dt),
            (cols_sb[:, 2, :], d_skip), (a_sb[:, :, :], a_log), (wo_sb[:, :, :], w_out),
            (wdt_sb[KP:KD, :], w_dt), (wx_sb[:, :, KP:KD], w_x[:, :, 0:RANK]),
        ] + [(wx_sb[:, :, r * NBC:(r + 1) * NBC], w_x[:, :, RANK:RANK + NBC]) for r in range(3)]
        n_weights = len(weight_loads)

        @block.sync
        def _(sp):
            def load(q):
                _, i, s = loads[q]
                old = q - RING
                if old >= 0:
                    if old in adds_at:
                        sp.wait_ge(adds_done, adds_at[old])
                    if old in blocks_at:
                        sp.wait_ge(blocks_done, blocks_at[old])
                    sp.wait_ge(ring_in[q % RING], 16 * (q // RING))
                sp.dma_start(ring[:, q % RING, :], adj[s, i]).then_inc(ring_in[q % RING], 16)

            for i in range(NS):
                for s in pass_a_order(i):
                    load(load_at["A", i, s])
                for b in range(BPS):
                    if i:
                        sp.wait_ge(adds_done, adds_per_strip * i)
                        sp.wait_ge(diag_done, i)
                        sp.wait_ge(diag_in[b], 16 * i)
                    sp.dma_start(diag[:, b, :], adj[BPS * i + b, i]).then_inc(diag_in[b], 16)
            for q, (phase, _, _) in enumerate(loads):
                if phase != "A":
                    load(q)

        @block.gpsimd
        def _(pool):
            nc.gpsimd.memset(ones[:, :], 1.0).then_inc(consts_done, 1)
            nc.gpsimd.memset(minus_half[:, :], -0.5).then_inc(consts_done, 1)
            nc.gpsimd.memset(state[:, :, :], 0.0).then_inc(consts_done, 1)

            def power(m, cols):
                pool.wait_ge(base_ready, m + 1)
                if m == 0:
                    pool.wait_ge(consts_done, 3)
                else:
                    pool.wait_ge(norm_ready, m)
                nc.gpsimd.tensor_tensor(rstd[:, 0:cols], base[:, 0:cols], minus_half[:, 0:cols],
                                        ALU.pow).then_inc(pow_done, 1)

            for m in range(3 * NS):
                power(m, TPS)

            for g in range(FIRST_SLOT, LAST_SLOT):
                k, n = divmod(g, DS)
                if n == 4 and 0 <= k + 1 < NCH:
                    power(3 * NS + k + 1, CT)
                if 0 <= k < NCH:
                    buf = hs[g % HSB]
                    pool.wait_ge(scan_done, 2 * (g + 1))
                    nc.gpsimd.tensor_copy(state[:, :, n:n + 1], buf[:, :, T - 1:T]).then_inc(state_saved, 1)
                    pool.wait_ge(state_saved, g + 1)
                    pool.wait_ge(c_copied, g + 1)
                    nc.gpsimd.tensor_tensor(buf, buf, csb[g % 2].unsqueeze(1).to_broadcast([P, HALVES, T]),
                                            ALU.mult).then_inc(mult_done, 1)
                    if n % 2:
                        pool.wait_ge(mult_done, g + 1)
                        even = hs[(g - 1) % HSB]
                        nc.gpsimd.tensor_tensor(even, even, buf, ALU.add).then_inc(pair_done, 1)

        @block.vector
        def _(dve):
            steps = [0]

            def step(ins):
                steps[0] += 1
                ins.then_inc(dve_step, 1)
                dve.wait_ge(dve_step, steps[0])

            powers = [0]

            def norm_stats(tiles):
                n = len(tiles)
                for t, v in enumerate(tiles):
                    ins = nc.vector.bn_stats(stats[:, t, :], v)
                step(ins)
                for t in range(n):
                    ins = nc.vector.bn_aggr(mv[:, t, :], stats[:, t, :])
                step(ins)
                powers[0] += 1
                nc.vector.tensor_scalar(base[:, 0:n], mv[:, 0:n, 1], LN_EPS, None, ALU.add).then_inc(base_ready, 1)

            def norm_bias(n):
                dve.wait_ge(pow_done, powers[0])
                nc.vector.scalar_tensor_tensor(nmr[:, 0:n], mv[:, 0:n, 0], -1.0, rstd[:, 0:n],
                                               ALU.mult, ALU.mult).then_inc(norm_ready, 1)

            dve.wait_ge(weights_in, 16 * n_weights)
            dve.wait_ge(consts_done, 3)
            for r in range(3):
                step(nc.vector.tensor_copy(pick[r * NBC:(r + 1) * NBC, :],
                                           ident[r * NBC:(r + 1) * NBC, r * NBC:(r + 1) * NBC]))
            dve.wait_ge(a_done, 1)
            step(nc.vector.tensor_scalar(a_sb[:, :, :], a_sb[:, :, :], -1.0, None, ALU.mult))
            total_adds = 0
            rowacc_blocks = rowacc
            for i in range(NS):
                order = [("ring", load_at["A", i, s]) for s in pass_a_order(i)] + [("diag", b) for b in range(BPS)]

                def arrived(where):
                    kind, q = where
                    if kind == "ring":
                        dve.wait_ge(ring_in[q % RING], 16 * (q // RING + 1))
                        return ring[:, q % RING, :]
                    dve.wait_ge(diag_in[q], 16 * (i + 1))
                    return diag[:, q, :]

                dve.wait_ge(xs_in[i % 2], 16 * (i // 2 + 1))
                if i:
                    dve.wait_ge(normed, i)
                norm_stats([tile_of(xs[i % 2], t) for t in range(TPS)])
                norm_bias(TPS)
                if i:
                    dve.wait_ge(fold_done, i)
                first, second = arrived(order[0]), arrived(order[1])
                total_adds += 1
                nc.vector.tensor_tensor(rowacc_blocks, first, second, ALU.add).then_inc(adds_done, 1)
                for where in order[2:]:
                    v = arrived(where)
                    dve.wait_ge(adds_done, total_adds)
                    total_adds += 1
                    nc.vector.tensor_tensor(rowacc_blocks, rowacc_blocks, v, ALU.add).then_inc(adds_done, 1)
                dve.wait_ge(fold_done, i + 1)
                dve.wait_ge(normed, i + 1)
                powers[0] += 1
                nc.vector.tensor_scalar(base[:, :], ps_deg, DEG_EPS, None, ALU.add).then_inc(base_ready, 1)
                dve.wait_ge(pow_done, powers[0])
                deg = dcol[:, i * TPS:(i + 1) * TPS]
                nc.vector.tensor_copy(deg, rstd[:, :]).then_inc(norm_ready, 1)
                dve.wait_ge(norm_ready, powers[0])
                hv = rows(h0[:, i * STRIP:(i + 1) * STRIP], TPS)
                nc.vector.tensor_tensor(hv, hv, deg.unsqueeze(2).to_broadcast([P, TPS, F]),
                                        ALU.mult).then_inc(h0_ready, 1)

            for n, i in enumerate(reversed(range(NS))):
                mine = part[:, i * STRIP:(i + 1) * STRIP]
                if n == 0:
                    dve.wait_ge(part_ready, NS)
                else:
                    dve.wait_ge(layer0_sum, n)
                    dve.wait_ge(w_done, n)
                    nc.vector.tensor_tensor(halves(s0), acc0[i % 2], halves(mine), ALU.add).then_inc(s0_ready, 1)
                dve.wait_ge(w_done, n + 1)
                deg = dcol[:, i * TPS:(i + 1) * TPS].unsqueeze(2).to_broadcast([P, TPS, F])
                pv = rows(pre, TPS)
                step(nc.vector.tensor_tensor(pv, ps_w.rearrange("p b (t f) -> p (b t) f", f=F), deg, ALU.mult))
                step(nc.vector.tensor_tensor(pv, pv, b0_sb[:, :].unsqueeze(1).to_broadcast([P, TPS, F]), ALU.add))
                dve.wait_ge(xs_in[n % 2], 16 * (NS // 2 + n // 2 + 1))
                if n >= 2:
                    dve.wait_ge(x1_out[n % 2], 16 * (n // 2))
                if n:
                    dve.wait_ge(normed, NS + n)
                nc.vector.scalar_tensor_tensor(x1[n % 2], pre, 0.0, xs[n % 2], ALU.max, ALU.add)\
                    .then_inc(x1_ready, 1)
                dve.wait_ge(x1_ready, n + 1)
                norm_stats([tile_of(x1[n % 2], t) for t in range(TPS)])
                norm_bias(TPS)

            for g in range(FIRST_SLOT, LAST_SLOT):
                k, n = divmod(g, DS)
                pk, qk = k + 1, k - 1
                if 0 <= k < NCH:
                    if n == 0:
                        dve.wait_ge(dt_ready, 2 * (k + 1))
                    dve.wait_ge(b_ready, g + 1)
                    if g:
                        dve.wait_ge(scan_done, 2 * g)
                    nc.vector.tensor_tensor(dbu, w[k % 2], b_ps[g % 2].unsqueeze(1).to_broadcast([P, HALVES, T]),
                                            ALU.mult).then_inc(dbu_done, 1)
                    dve.wait_ge(dbu_done, g + 1)
                    dve.wait_ge(da_ready, g + 1)
                    if k:
                        dve.wait_ge(state_saved, g - DS + 1)
                    if g // 2 >= HSB // 2:
                        dve.wait_ge(nsum_done, g // 2 - HSB // 2 + 1)
                    for h in range(HALVES):
                        nc.vector.tensor_tensor_scan(hs[g % HSB][:, h, :], da[g % 2][:, h, :], dbu[:, h, :],
                                                     state[:, h, n:n + 1], ALU.mult, ALU.add).then_inc(scan_done, 1)
                if n == 2 and pk < NCH and pk % CPS == 0:
                    i = pk // CPS
                    dve.wait_ge(blocks_done, blocks_at[load_at["C", i, BPS * (i + 1) - 1]])
                    if i < NS - 1:
                        dve.wait_ge(l1_back, 16 * (i + 1))
                        nc.vector.tensor_tensor(halves(s1), acc_c, halves(l1_part), ALU.add).then_inc(s1_ready, 1)
                    else:
                        dve.wait_ge(misc_full, misc_at["gcn", pk - 1] + 1)
                        nc.vector.tensor_copy(halves(s1), acc_c).then_inc(s1_ready, 1)
                if n == 3 and 0 <= qk < NCH:
                    dve.wait_ge(nsum_done, DS // 2 * (qk + 1))
                    if qk:
                        dve.wait_ge(misc_full, misc_at["out", qk - 1] + 1)
                    for h in range(HALVES):
                        ins = nc.vector.scalar_tensor_tensor(yg[:, h, :], u[qk % 2][:, h, :], cols_sb[:, 2, h:h + 1],
                                                             y_ps[:, h, :], ALU.mult, ALU.add)
                    ins.then_inc(y_free, 1)
                    dve.wait_ge(y_free, qk + 1)
                    nc.vector.tensor_tensor(yg, yg, sz[qk % 2], ALU.mult).then_inc(yg_ready, 1)
                if n == 4 and pk < NCH:
                    dve.wait_ge(misc_full, misc_at["gcn", pk] + 1)
                    if pk:
                        dve.wait_ge(misc_full, misc_at["tr", pk - 1] + 1)
                    nc.vector.tensor_tensor(gbuf, rows(m_ps, CT), gb_sb[:, :].unsqueeze(1).to_broadcast([P, CT, F]),
                                            ALU.add).then_inc(misc_free, 1)
                    dve.wait_ge(misc_free, misc_at["gcn", pk] + 1)
                    step(nc.vector.tensor_scalar(gbuf, gbuf, 0.0, None, ALU.max))
                    dve.wait_ge(normed, NORM_C + pk)
                    norm_stats([gbuf[:, t, :] for t in range(CT)])
                if n == 5 and pk < NCH:
                    norm_bias(CT)
                if n == 5 and 0 <= qk < NCH:
                    dve.wait_ge(misc_full, misc_at["out", qk] + 1)
                    dve.wait_ge(x1t_in[qk % 2], 16 * (qk // 2 + 1))
                    nc.vector.tensor_tensor(x1t[qk % 2], rows(m_ps, CT), x1t[qk % 2], ALU.add)\
                        .then_inc(misc_free, 1)
                if n in (8, 9) and pk < NCH:
                    h = n - 8
                    xc = xcp[pk % 2][:, h, :]
                    if pk:
                        ins = nc.vector.tensor_copy(xc[:, 1:CONV], xcp[(pk - 1) % 2][:, h, T + 1:T + CONV])
                    else:
                        ins = nc.vector.memset(xc[:, 1:CONV], 0.0)
                    step(ins)
                    evacuated(dve, f"xz{h}", pk)
                    acc = cv[:, h, :]
                    step(nc.vector.tensor_scalar(acc, xc[:, 1:1 + T], conv_sb[:, h, 0:1], cols_sb[:, 0, h:h + 1],
                                                 ALU.mult, ALU.add))
                    for tap in range(1, CONV):
                        ins = nc.vector.scalar_tensor_tensor(acc, xc[:, 1 + tap:1 + tap + T],
                                                             conv_sb[:, h, tap:tap + 1], acc, ALU.mult, ALU.add)
                        if tap < CONV - 1:
                            step(ins)
                    ins.then_inc(conv_done, 1)
                if n == 12 and pk < NCH:
                    pb = parts[pk % 2]
                    evacuated(dve, "dbc", pk)
                    step(nc.vector.tensor_copy(pb[:, :], bcv[0:KP, :]))
                    step(nc.vector.tensor_tensor(bcv[0:KP, :], bcv[0:KP, :], pb[:, :], ALU.subtract))
                    for r in (1, 2):
                        ins = nc.vector.tensor_copy(pb[r * NBC:(r + 1) * NBC, :], bcv[r * NBC:(r + 1) * NBC, :])
                    step(ins)
                    third = slice(2 * NBC, 3 * NBC)
                    step(nc.vector.tensor_tensor(bcv[third, :], bcv[third, :], pb[third, :], ALU.subtract))
                    nc.vector.tensor_copy(pb[third, :], bcv[third, :]).then_inc(parts_ready, 1)
                ex, w1 = w[pk % 2], dt[pk % 2]
                if n == 13 and pk < NCH:
                    dve.wait_ge(ex_ready, pk + 1)
                    step(nc.vector.tensor_scalar(w1, ex, 1.0, None, ALU.add))
                    nc.vector.scalar_tensor_tensor(ex, w1, -1.0, ex, ALU.add, ALU.subtract).then_inc(w1_ready, 1)
                    dve.wait_ge(w1_ready, pk + 1)
                    step(nc.vector.scalar_tensor_tensor(ex, cv, 0.0, ex, ALU.max, ALU.subtract))
                if n == 14 and pk < NCH:
                    dve.wait_ge(log_ready, pk + 1)
                    nc.vector.tensor_tensor(dt[pk % 2], ex, w1, ALU.add).then_inc(dt_ready, 1)
                    dve.wait_ge(dt_ready, 2 * pk + 1)
                    dve.wait_ge(u_ready, pk + 1)
                    nc.vector.tensor_tensor(w[pk % 2], dt[pk % 2], u[pk % 2], ALU.mult).then_inc(dt_ready, 1)

        @block.tensor
        def _(pe):
            def arrived(q):
                pe.wait_ge(ring_in[q % RING], 16 * (q // RING + 1))
                return ring[:, q % RING, :]

            def product(acc, h, s, blk, start, stop, todo=None):
                for a in range(JT):
                    for c in range(STRIP // MM):
                        last = nc.tensor.matmul(acc[:, c, :], tile_of(h, JT * s + a),
                                                blk[:, a * STRIP + c * MM:a * STRIP + (c + 1) * MM],
                                                start=start and a == 0, stop=stop and a == JT - 1)
                return last

            pe.wait_ge(consts_done, 3)
            for i in range(NS):
                if i >= 2:
                    pe.wait_ge(part_ready, i - 1)
                first = True
                for s in pass_a_order(i):
                    if s < BPS * i:
                        pe.wait_ge(h0_ready, s // BPS + 1)
                        product(acc0[i % 2], h0, s, arrived(load_at["A", i, s]), first, False)\
                            .then_inc(blocks_done, 1)
                        first = False
                pe.wait_ge(adds_done, adds_per_strip * (i + 1))
                if i:
                    pe.wait_ge(h0_ready, i)
                for t in range(TPS):
                    for a in range(JT):
                        last = nc.tensor.matmul(ps_deg[:, t:t + 1],
                                                rowacc[:, a * STRIP + t * P:a * STRIP + (t + 1) * P], ones[:, :],
                                                start=a == 0, stop=a == JT - 1)
                last.then_inc(fold_done, 1)
                pe.wait_ge(h0_ready, i + 1)
                for b in range(BPS):
                    pe.wait_ge(diag_in[b], 16 * (i + 1))
                    last = product(acc0[i % 2], h0, BPS * i + b, diag[:, b, :], first, b == BPS - 1)
                    first = False
                last.then_inc(diag_done, 1)

            def through_w(n, i):
                if n == 0:
                    pe.wait_ge(part_ready, NS)
                    src = part[:, i * STRIP:(i + 1) * STRIP]
                else:
                    pe.wait_ge(s0_ready, n)
                    pe.wait_ge(x1_ready, n)
                    src = s0
                for t in range(TPS):
                    last = nc.tensor.matmul(ps_w[:, t // CT, t % CT * F:(t % CT + 1) * F],
                                            src[:, t * P:(t + 1) * P], w0t_sb[:, :], start=True, stop=True)
                last.then_inc(w_done, 1)

            pe.wait_ge(weights_in, 16 * n_weights)
            through_w(0, NS - 1)
            for n, i in enumerate(reversed(range(NS - 1))):
                blocks = list(reversed(range(BPS * (i + 1), NB)))
                jobs = []
                for m, s in enumerate(blocks):
                    jobs.append((0, s))
                    if m == 0 and n:
                        jobs.append(("w", None))
                    if m < len(blocks) - BPS:
                        jobs.append((1, s))
                jobs += [(1, s) for s in blocks[-BPS:]]
                for layer, s in jobs:
                    if layer == "w":
                        through_w(n, i + 1)
                        continue
                    q = load_at["B", i, s]
                    blk = arrived(q)
                    if layer == 0:
                        if s == blocks[0]:
                            if n < 2:
                                pe.wait_ge(part_ready, NS)
                            else:
                                pe.wait_ge(s0_ready, n - 1)
                        last = product(acc0[i % 2], h0, s, blk, s == blocks[0], s == blocks[-1])
                        if s == blocks[-1]:
                            last.then_inc(layer0_sum, 1)
                    else:
                        pe.wait_ge(normed, NS + NS - s // BPS)
                        if s == blocks[0] and n:
                            pe.wait_ge(l1_staged, n)
                        product(acc1, h1, s, blk, s == blocks[0], s == blocks[-1]).then_inc(blocks_done, 1)
            through_w(NS - 1, 0)

            def c_products(mms):
                for i, s, a, c in mms:
                    q = load_at["C", i, s]
                    blk = arrived(q) if (a, c) == (0, 0) else ring[:, q % RING, :]
                    if (s, a, c) == (0, 0, 0):
                        pe.wait_ge(normed, NORM_C)
                        if i:
                            pe.wait_ge(s1_ready, i)
                    last = nc.tensor.matmul(acc_c[:, c, :], tile_of(h1, JT * s + a),
                                            blk[:, a * STRIP + c * MM:a * STRIP + (c + 1) * MM],
                                            start=s == 0 and a == 0, stop=s == BPS * (i + 1) - 1 and a == JT - 1)
                    if (a, c) == (JT - 1, STRIP // MM - 1):
                        last.then_inc(blocks_done, 1)

            def use_misc(key):
                m = misc_at[key]
                if m:
                    pe.wait_ge(misc_free, m)

            c_products(products[FIRST_SLOT - 1])
            for g in range(FIRST_SLOT, LAST_SLOT):
                k, n = divmod(g, DS)
                pk, qk = k + 1, k - 1
                if 0 <= g + 1 < NCH * DS:
                    kk, nn = divmod(g + 1, DS)
                    pe.wait_ge(parts_ready, kk + 1)
                    if g + 1 >= 2:
                        pe.wait_ge(dbu_done, g)
                    pv = parts[kk % 2]
                    nc.tensor.matmul(b_ps[(g + 1) % 2], pick[:, nn:nn + 1].to_broadcast([KP, P]), pv[:, :],
                                     start=True, stop=True).then_inc(b_ready, 1)
                    if g + 1:
                        pe.wait_ge(c_copied, g + 1)
                    nc.tensor.matmul(c_ps, pick[:, DS + nn:DS + nn + 1].to_broadcast([KP, P]), pv[:, :],
                                     start=True, stop=True).then_inc(c_ready, 1)
                G, odd = divmod(g - 4, 2)
                if not odd and 0 <= G < NCH * DS // 2:
                    pe.wait_ge(pair_done, G + 1)
                    first = G % (DS // 2) == 0
                    if first and G:
                        pe.wait_ge(y_free, G // (DS // 2))
                    if G == 0:
                        pe.wait_ge(normed, NORM_C)
                    for h in range(HALVES):
                        last = nc.tensor.matmul(y_ps[:, h, :], ident[:, :], hs[2 * G % HSB][:, h, :],
                                                start=first, stop=G % (DS // 2) == DS // 2 - 1)
                    last.then_inc(nsum_done, 1)
                if pk < NCH:
                    if n == 3:
                        pe.wait_ge(s1_ready, pk // CPS + 1)
                        use_misc(("gcn", pk))
                        for t in range(CT):
                            c = pk % CPS * T + t * P
                            last = nc.tensor.matmul(m_ps[:, t * F:(t + 1) * F], s1[:, c:c + P], gw_sb[:, :],
                                                    start=True, stop=True)
                        last.then_inc(misc_full, 1)
                if n == 5 and 0 <= qk < NCH:
                    pe.wait_ge(yg_ready, qk + 1)
                    use_misc(("out", qk))
                    for t in range(CT):
                        for h in range(HALVES):
                            last = nc.tensor.matmul(m_ps[:, t * F:(t + 1) * F], yg[:, h, t * P:(t + 1) * P],
                                                    wo_sb[:, h, :], start=h == 0, stop=h == HALVES - 1)
                    last.then_inc(misc_full, 1)
                if pk < NCH:
                    if n == 6:
                        pe.wait_ge(normed, NORM_C + pk + 1)
                        use_misc(("tr", pk))
                        for t in range(CT):
                            last = nc.tensor.transpose(m_ps[:, t * P:(t + 1) * P], gbuf[:, t, :], ident[:, :])
                        last.then_inc(misc_full, 1)
                    if 7 <= n <= 10:
                        c = n - 7
                        evacuated(pe, "tr", pk)
                        use_misc((f"xz{c}", pk))
                        nc.tensor.matmul(m_ps, w_in_sb[:, c * P:(c + 1) * P], h_t, start=True, stop=True)\
                            .then_inc(misc_full, 1)
                    if n == 11:
                        pe.wait_ge(u_ready, pk + 1)
                        use_misc(("dbc", pk))
                        for h in range(HALVES):
                            last = nc.tensor.matmul(m_ps[0:KD, :], wx_sb[:, h, :], u[pk % 2][:, h, :],
                                                    start=h == 0, stop=h == HALVES - 1)
                        last.then_inc(misc_full, 1)
                    if n == 12:
                        for h in range(HALVES):
                            evacuated(pe, "dbc", pk)
                            use_misc((f"dt{h}", pk))
                            nc.tensor.matmul(m_ps, wdt_sb[KP:KD, h * P:(h + 1) * P], bcv[KP:KD, :],
                                             start=True, stop=True).then_inc(misc_full, 1)
                c_products(products[g])

        @block.scalar
        def _(act):
            for dst, src in weight_loads:
                act.dma_start(dst, src).then_inc(weights_in, 16)

            def load_xs(n, i):
                act.dma_start(xs[n % 2], x[:, i * STRIP:(i + 1) * STRIP]).then_inc(xs_in[n % 2], 16)

            def normalise(src, dst, n, func):
                for t in range(n):
                    last = nc.scalar.activation(dst[t], src[t], func, bias=nmr[:, t:t + 1], scale=rstd[:, t:t + 1])
                last.then_inc(normed, 1)

            load_xs(0, 0)
            load_xs(1, 1)
            act.wait_ge(weights_in, 16 * n_weights)
            nc.scalar.activation(a_sb[:, :, :], a_sb[:, :, :], ACT.Exp).then_inc(a_done, 1)

            def move_part(i):
                act.wait_ge(diag_done, i + 1)
                nc.scalar.activation(halves(part[:, i * STRIP:(i + 1) * STRIP]), acc0[i % 2], ACT.Copy).then_inc(part_ready, 1)

            for i in range(NS):
                act.wait_ge(norm_ready, 2 * i + 1)
                normalise([tile_of(xs[i % 2], t) for t in range(TPS)],
                          [tile_of(h0, i * TPS + t) for t in range(TPS)], TPS, ACT.Relu)
                act.wait_ge(normed, i + 1)
                m = i + 2
                load_xs(m, m if m < NS else 2 * NS - 1 - m)
                if i:
                    move_part(i - 1)
            move_part(NS - 1)

            for n, i in enumerate(reversed(range(NS))):
                if n:
                    act.wait_ge(blocks_done, blocks_at[load_at["B", i, BPS * (i + 1)]])
                    if n > 1:
                        act.wait_ge(l1_out, 16 * (n - 1))
                    nc.scalar.activation(halves(l1_stage), acc1, ACT.Copy).then_inc(l1_staged, 1)
                    act.wait_ge(l1_staged, n)
                    act.dma_start(upper1_dram[:, i * STRIP:(i + 1) * STRIP], l1_stage).then_inc(l1_out, 16)
                act.wait_ge(norm_ready, 2 * NS + n + 1)
                if n == 0:
                    act.wait_ge(diag_done, NS)
                normalise([tile_of(x1[n % 2], t) for t in range(TPS)],
                          [tile_of(h1, i * TPS + t) for t in range(TPS)], TPS, ACT.Relu)
                act.dma_start(x1_dram[:, i * STRIP:(i + 1) * STRIP], x1[n % 2]).then_inc(x1_out[n % 2], 16)
                m = n + 2
                if m < NS:
                    act.wait_ge(x1_ready, n + 1)
                    load_xs(m, NS - 1 - m)

            def load_x1t(k):
                act.dma_start(x1t[k % 2], rows(x1_dram[:, k * T:(k + 1) * T], CT)).then_inc(x1t_in[k % 2], 16)

            for b in range(2):
                act.wait_ge(x1_out[b], 16 * NS // 2)
            act.wait_ge(l1_out, 16 * (NS - 1))
            act.wait_ge(w_done, NS)
            act.wait_ge(normed, NORM_C)
            for g in range(FIRST_SLOT, LAST_SLOT):
                k, n = divmod(g, DS)
                pk, qk = k + 1, k - 1
                if 0 <= g + 1 < NCH * DS:
                    kk, nn = divmod(g + 1, DS)
                    act.wait_ge(c_ready, g + 2)
                    if g + 1 >= 2:
                        act.wait_ge(mult_done, g)
                    nc.scalar.activation(csb[(g + 1) % 2], c_ps, ACT.Copy).then_inc(c_copied, 1)
                    if nn == 0:
                        act.wait_ge(dt_ready, 2 * kk + 1)
                    if g + 1 >= 2:
                        act.wait_ge(scan_done, 2 * g)
                    for h in range(HALVES):
                        last = nc.scalar.activation(da[(g + 1) % 2][:, h, :], dt[kk % 2][:, h, :], ACT.Exp,
                                                    scale=a_sb[:, h, nn:nn + 1])
                    last.then_inc(da_ready, 1)
                if n == 0 and pk < NCH and pk % CPS == 0 and pk // CPS < NS - 1:
                    i = pk // CPS
                    if pk:
                        act.wait_ge(misc_full, misc_at["gcn", pk - 1] + 1)
                    act.dma_start(l1_part, upper1_dram[:, i * STRIP:(i + 1) * STRIP]).then_inc(l1_back, 16)
                if n == 1 and 0 <= k < NCH:
                    if k >= 2:
                        act.wait_ge(out_done[k % 2], 16 * (k // 2))
                    load_x1t(k)
                ex, w1 = w[pk % 2], dt[pk % 2]
                if pk < NCH:
                    def evacuate(key, dst, src, **more):
                        act.wait_ge(misc_full, misc_at[key] + 1)
                        nc.scalar.activation(dst, src, ACT.Identity if more else ACT.Copy, **more)\
                            .then_inc(misc_free, 1)

                    if n == 5:
                        act.wait_ge(norm_ready, 3 * NS + pk + 1)
                        g4 = [gbuf[:, t, :] for t in range(CT)]
                        normalise(g4, g4, CT, ACT.Identity)
                    if n == 6:
                        evacuate(("tr", pk), h_t, m_ps, scale=ln_sb[:, 0:1], bias=ln_sb[:, 1:2])
                    if n in (7, 8):
                        if pk >= 2:
                            act.wait_ge(conv_done, HALVES * pk)
                        evacuate((f"xz{n - 7}", pk), xcp[pk % 2][:, n - 7, CONV:CONV + T], m_ps)
                    if n in (9, 10):
                        if pk >= 2:
                            act.wait_ge(yg_ready, pk - 1)
                        evacuate((f"xz{n - 7}", pk), sz[pk % 2][:, n - 9, :], m_ps)
                    if n == 10:
                        act.wait_ge(conv_done, HALVES * (pk + 1))
                        nc.scalar.activation(u[pk % 2], cv, ACT.Silu).then_inc(u_ready, 1)
                        evacuated(act, "xz3", pk)
                        nc.scalar.activation(sz[pk % 2], sz[pk % 2], ACT.Silu).then_inc(sz_ready, 1)
                    if n == 11:
                        evacuate(("dbc", pk), bcv[0:KD, :], m_ps[0:KD, :])
                    if n == 12:
                        for h in range(HALVES):
                            evacuate((f"dt{h}", pk), cv[:, h, :], m_ps, bias=cols_sb[:, 1, h:h + 1],
                                     scale=1.0)
                        evacuated(act, "dt1", pk)
                        nc.scalar.activation(ex, cv, ACT.Abs).then_inc(act_step, 1)
                        act.wait_ge(act_step, pk + 1)
                        nc.scalar.activation(ex, ex, ACT.Exp, scale=-1.0).then_inc(ex_ready, 1)
                    if n == 13:
                        act.wait_ge(w1_ready, pk + 1)
                        nc.scalar.activation(w1, w1, ACT.Ln).then_inc(log_ready, 1)
                if n == 6 and 0 <= qk < NCH:
                    act.wait_ge(misc_free, misc_at["out", qk] + 1)
                    act.dma_start(rows(out[:, qk * T:(qk + 1) * T], CT), x1t[qk % 2]).then_inc(out_done[qk % 2], 16)
            for b in range(2):
                act.wait_ge(out_done[b], 16 * NCH // 2)


def kernel(x, adj, L0_gnn_W, L0_gnn_b, L1_gnn_gcn_w, L1_gnn_gcn_b, L1_gnn_ln_g, L1_gnn_ln_b, L1_gnn_w_in,
           L1_gnn_conv_w, L1_gnn_conv_b, L1_gnn_w_xp, L1_gnn_w_dt, L1_gnn_b_dt, L1_gnn_A_log, L1_gnn_D_skip,
           L1_gnn_w_out):
    import numpy as np
    import concourse.bacc as bacc
    from concourse.bass_utils import run_bass_kernel_spmd

    def by_halves(a):
        a = np.asarray(a)
        return a.reshape(HALVES, P, -1).transpose(1, 0, 2)

    def column(a):
        return np.asarray(a).reshape(P, 1)

    laid_out = {
        "adj": np.asarray(adj).reshape(NS, STRIP, NB, JT, P).transpose(2, 0, 4, 3, 1).reshape(NB, NS, P, BLOCK),
        "x": np.asarray(x).reshape(N // P, P, F).transpose(1, 0, 2).reshape(P, N),
        "w0t": np.asarray(L0_gnn_W).T,
        "b0": np.asarray(L0_gnn_b).reshape(1, F),
        "gcn_w": L1_gnn_gcn_w,
        "gcn_b": np.asarray(L1_gnn_gcn_b).reshape(1, F),
        "ln_g": column(L1_gnn_ln_g),
        "ln_b": column(L1_gnn_ln_b),
        "w_in": L1_gnn_w_in,
        "conv_w": by_halves(L1_gnn_conv_w),
        "conv_b": by_halves(L1_gnn_conv_b)[:, :, 0],
        "w_x": by_halves(L1_gnn_w_xp),
        "w_dt": L1_gnn_w_dt,
        "b_dt": by_halves(L1_gnn_b_dt)[:, :, 0],
        "a_log": by_halves(L1_gnn_A_log),
        "d_skip": by_halves(L1_gnn_D_skip)[:, :, 0],
        "w_out": by_halves(L1_gnn_w_out),
        "ident_in": np.eye(P, dtype=np.float32),
    }
    nc = bacc.Bacc("TRN2", target_bir_lowering=False, num_devices=1)
    arrays, args = {}, {}
    for name, a in laid_out.items():
        arrays[name] = np.ascontiguousarray(a)
        args[name] = nc.dram_tensor(name, arrays[name].shape, F32, kind="ExternalInput").ap()
    out = nc.dram_tensor("out", (P, N), F32, kind="ExternalOutput").ap()
    build(nc, out=out, **args)
    got = run_bass_kernel_spmd(nc, [arrays], core_ids=[0]).results[0]["out"]
    return np.ascontiguousarray(got.reshape(P, N // P, F).transpose(1, 0, 2).reshape(N, F))
```

```python
from contextlib import ExitStack

import concourse.bass as bass
from concourse import mybir

P = 128
N = 8192
F = 128
DI = 256
DS = 16
RANK = 8
HALVES = DI // P
STRIP = 1024
NS = N // STRIP
TPS = STRIP // P
BJ = 256
JT = BJ // P
NB = N // BJ
BPS = STRIP // BJ
BLOCK = JT * STRIP
MM = 512
RING = 7
T = 512
NCH = N // T
ARENA = 26 * STRIP
CPS = STRIP // T
CT = T // P
NBC = 2 * DS
KP = 3 * NBC
KD = KP + RANK
CONV = 4
LN_EPS = 1e-5
DEG_EPS = 1e-9
HSB = 4
AHEAD = 4

F32 = mybir.dt.float32
F32R = mybir.dt.float32r
BF16 = mybir.dt.bfloat16
ALU = mybir.AluOpType
ACT = mybir.ActivationFunctionType


def pass_a_order(i):
    lower, upper = list(range(BPS * i)), list(range(BPS * (i + 1), NB))
    total, products = len(lower) + len(upper), len(lower)
    return [(lower if (n + 1) * products // total > n * products // total else upper).pop(0) for n in range(total)]


def build(nc, adj, x, w0t, b0, gcn_w, gcn_b, ln_g, ln_b, w_in, conv_w, conv_b, w_x, w_dt, b_dt, a_log, d_skip,
          w_out, ident_in, out):
    x1_dram = nc.dram_tensor("x1_scratch", (P, N // P * F), F32, kind="Internal").ap()
    lower0_dram = nc.dram_tensor("lower0_scratch", (P, N), F32, kind="Internal").ap()
    c_dram = nc.dram_tensor("c_scratch", (NCH, DS * T), F32, kind="Internal").ap()
    upper1_dram = nc.dram_tensor("upper1_scratch", (P, N), F32, kind="Internal").ap()

    loads = [("A", i, s) for i in range(NS) for s in pass_a_order(i)]
    loads += [("B", i, s) for i in reversed(range(NS)) for s in reversed(range(BPS * (i + 1), NB))]
    loads += [("C", i, s) for i in range(NS) for s in range(BPS * (i + 1))]
    load_at = {key: q for q, key in enumerate(loads)}

    adds_at, blocks_at = {}, {}
    adds = blocks = 0
    for i in range(NS):
        for n, s in enumerate(pass_a_order(i)):
            adds += n > 0
            adds_at[load_at["A", i, s]] = adds + (n == 0)
            if s < BPS * i:
                blocks += 1
                blocks_at[load_at["A", i, s]] = blocks
        adds += BPS
    adds_per_strip = NB - 1
    assert adds == NS * adds_per_strip
    pieces_at = {}
    pieces = 0
    for q, (phase, _, _) in enumerate(loads):
        if phase == "B":
            pieces += JT
            pieces_at[q] = pieces
        if phase == "C":
            blocks += 1
            blocks_at[q] = blocks

    FIRST_SLOT, LAST_SLOT = -DS, NCH * DS + 8
    slots = list(range(FIRST_SLOT - 1, LAST_SLOT))
    products = {g: [] for g in slots}
    mms = [[(i, s, a, c) for s in range(BPS * (i + 1)) for a in range(JT) for c in range(STRIP // MM)]
           for i in range(NS)]
    products[FIRST_SLOT - 1] = mms[0]
    handover = {0: FIRST_SLOT + 2}
    start, end = FIRST_SLOT + 2, DS * (CPS * (NS - 1) - 1) + 2
    total, n = sum(len(m) for m in mms[1:]), 0
    for i in range(1, NS):
        for mm in mms[i]:
            products[max(start + n * (end - start) // total, handover[i - 1])].append(mm)
            n += 1
        handover[i] = min(start + n * (end - start) // total + 1, end)
        assert handover[i] <= DS * (CPS * i - 1) + 2
        assert i < 2 or handover[i] > DS * (CPS * (i - 1) - 2) + 4
    block_end = {load_at["C", i, s]: g for g in slots for i, s, _, _ in products[g]}

    misc = []
    for g in range(FIRST_SLOT, LAST_SLOT):
        k, n = divmod(g, DS)
        if n == 5 and 0 <= k - 1 < NCH:
            misc.append(("out", k - 1))
        if 0 <= k + 1 < NCH:
            misc += {3: [("gcn", k + 1)], 6: [("tr", k + 1)], 7: [("xz0", k + 1)], 8: [("xz1", k + 1)],
                     9: [("xz2", k + 1)], 10: [("xz3", k + 1)], 11: [("dbc", k + 1)],
                     12: [("dt0", k + 1), ("dt1", k + 1)]}.get(n, [])
    misc_at = {key: m for m, key in enumerate(misc)}

    with ExitStack() as ctx:
        def sb(name, shape, dt=F32):
            return ctx.enter_context(nc.sbuf_tensor(name, shape, dt))

        def sem(name):
            return ctx.enter_context(nc.semaphore(name))

        ring = sb("ring", [P, RING, BLOCK])
        diag_h1 = sb("diag_h1", [P, BPS * BLOCK])
        diag = diag_h1[:, :].rearrange("p (b c) -> p b c", b=BPS)
        h1 = diag_h1[:, 0:N]
        arena_offset = nc.sbuf_base
        arena = sb("arena", [P, ARENA])
        h0 = arena[:, 0:N]
        adj_parts = nc.alloc_sbuf_tensor_at("adj_parts", [P, 2, 2, STRIP], F32R, offset=arena_offset + 4 * N)
        h_parts = nc.alloc_sbuf_tensor_at("h_parts", [P, 2, 2, 2, JT * F], F32R,
                                          offset=arena_offset + 4 * (N + 4 * STRIP))
        top = [N + 4 * STRIP + 8 * JT * F]

        def work(cols):
            top[0] += cols
            assert top[0] <= ARENA
            return arena[:, top[0] - cols:top[0]]

        l0_sums = [work(STRIP) for _ in range(2)]
        xs = [work(STRIP) for _ in range(2)]
        after_xs = top[0]
        rowacc = work(BLOCK)
        top[0] = after_xs
        s0 = work(STRIP)
        pre = work(STRIP)
        x1 = [work(STRIP) for _ in range(2)]
        l1_stage = work(STRIP)
        top[0] = 0

        def work2(*dims):
            size = 1
            for d in dims:
                size *= d
            v = work(size)
            if len(dims) == 2:
                v = v.rearrange("p (a b) -> p a b", a=dims[0])
            return v

        s1 = [work2(STRIP) for _ in range(2)]
        gbuf = work2(CT, F)
        h_t = work2(T)
        xcp = [work2(HALVES, T + CONV) for _ in range(2)]
        cv = work2(HALVES, T)
        u = [work2(HALVES, T) for _ in range(2)]
        sz = [work2(HALVES, T) for _ in range(2)]
        bcv = work2(T)
        dt = [work2(HALVES, T) for _ in range(2)]
        w = [work2(HALVES, T) for _ in range(2)]
        da = [work2(HALVES, T) for _ in range(2)]
        dbu = work2(HALVES, T)
        hs = [work2(HALVES, T) for _ in range(HSB)]
        csb = [work2(2, T) for _ in range(2)]
        yg = work2(HALVES, T)
        x1t = [work2(CT, F) for _ in range(2)]
        parts = [sb(f"parts{i}", [KP, T], BF16) for i in range(2)]

        ident = sb("ident", [P, P])
        pick = sb("pick", [KP, NBC], BF16)
        ones = sb("ones", [P, 1])
        w0t_sb = sb("w0t_sb", [P, F])
        b0_sb = sb("b0_sb", [P, F])
        gw_sb = sb("gw_sb", [P, F])
        gb_sb = sb("gb_sb", [P, F])
        ln_sb = sb("ln_sb", [P, 2])
        w_in_sb = sb("w_in_sb", [P, 2 * DI])
        conv_sb = sb("conv_sb", [P, HALVES, CONV])
        cols_sb = sb("cols_sb", [P, 3, HALVES])
        wx_sb = sb("wx_sb", [P, HALVES, KD])
        wdt_sb = sb("wdt_sb", [P, DI])
        a_sb = sb("a_sb", [P, HALVES, DS])
        wo_sb = sb("wo_sb", [P, HALVES, F])
        state = sb("state", [P, HALVES, DS])
        dcol = sb("dcol", [P, N // P])
        stats = sb("stats", [P, TPS, 6])
        mv = sb("mv", [P, TPS, 2])
        base = sb("base", [P, TPS])
        minus_half = sb("minus_half", [P, TPS])
        rstd = sb("rstd", [P, TPS])
        nmr = sb("nmr", [P, TPS])

        ps = ctx.enter_context(nc.psum_tensor("ps", [P, 8, MM], F32))
        acc0 = [ps[:, 0:2, :], ps[:, 2:4, :]]
        ps_deg = ps[:, 4, 0:TPS]
        acc1 = ps[:, 4:6, :]
        ps_w = ps[:, 6:8, :]
        acc_c = ps[:, 2:4, :]
        y_ps = ps[:, 0:2, :]
        b_ps = [ps[:, 4, :], ps[:, 5, :]]
        misc_ps = [ps[:, 6, :], ps[:, 7, :]]

        weights_in = sem("weights_in")
        ring_in = [sem(f"ring_in{i}") for i in range(RING)]
        diag_in = [sem(f"diag_in{i}") for i in range(BPS)]
        xs_in = [sem(f"xs_in{i}") for i in range(2)]
        consts_done = sem("consts_done")
        a_done = sem("a_done")
        dve_step = sem("dve_step")
        adds_done = sem("adds_done")
        blocks_done = sem("blocks_done")
        diag_done = sem("diag_done")
        fold_done = sem("fold_done")
        base_ready = sem("base_ready")
        pow_done = sem("pow_done")
        norm_ready = sem("norm_ready")
        normed = sem("normed")
        h0_ready = sem("h0_ready")
        part_ready = sem("part_ready")
        layer0_sum = sem("layer0_sum")
        s0_ready = sem("s0_ready")
        w_done = sem("w_done")
        x1_ready = sem("x1_ready")
        x1_out = [sem(f"x1_out{i}") for i in range(2)]
        l1_staged = sem("l1_staged")
        l1_out = sem("l1_out")
        l1_back = [sem(f"l1_back{i}") for i in range(2)]
        l0_out = [sem(f"l0_out{i}") for i in range(2)]
        l0_back = [sem(f"l0_back{i}") for i in range(2)]
        hi_ready = sem("hi_ready")
        lo_ready = sem("lo_ready")
        h_hi_ready = sem("h_hi_ready")
        h_lo_ready = sem("h_lo_ready")
        pieces_done = sem("pieces_done")
        s1_ready = sem("s1_ready")
        misc_full = sem("misc_full")
        misc_free = [sem(f"misc_free{i}") for i in range(2)]
        act_step = sem("act_step")
        conv_done = sem("conv_done")
        u_ready = sem("u_ready")
        sz_ready = sem("sz_ready")
        parts_ready = sem("parts_ready")
        ex_ready = sem("ex_ready")
        w1_ready = sem("w1_ready")
        log_ready = sem("log_ready")
        dt_ready = sem("dt_ready")
        b_ready = sem("b_ready")
        c_out = sem("c_out")
        c_in = [sem(f"c_in{i}") for i in range(2)]
        da_ready = sem("da_ready")
        dbu_done = sem("dbu_done")
        scan_done = sem("scan_done")
        state_saved = sem("state_saved")
        mult_done = sem("mult_done")
        pair_done = sem("pair_done")
        nsum_done = sem("nsum_done")
        y_free = sem("y_free")
        yg_ready = sem("yg_ready")
        x1t_in = [sem(f"x1t_in{i}") for i in range(2)]
        o_ready = sem("o_ready")
        out_done = [sem(f"out_done{i}") for i in range(2)]

        NORM_C = 2 * NS

        block = ctx.enter_context(nc.Block())

        def tile_of(h, t):
            return h[:, t * F:(t + 1) * F]

        def rows(v, n):
            return v.rearrange("p (t f) -> p t f", t=n)

        def halves(v):
            return v.rearrange("p (h c) -> p h c", c=MM)

        def misc_of(kind, k):
            return misc_ps[misc_at[kind, k] % 2]

        def evacuated(eng, kind, k):
            m = misc_at[kind, k]
            eng.wait_ge(misc_free[m % 2], m // 2 + 1)

        weight_loads = [
            (ident[:, :], ident_in), (w0t_sb[:, :], w0t), (b0_sb[:, :], b0.to_broadcast([P, F])),
            (gw_sb[:, :], gcn_w), (gb_sb[:, :], gcn_b.to_broadcast([P, F])),
            (ln_sb[:, 0:1], ln_g), (ln_sb[:, 1:2], ln_b), (w_in_sb[:, :], w_in),
            (conv_sb[:, :, :], conv_w), (cols_sb[:, 0, :], conv_b), (cols_sb[:, 1, :], b_dt),
            (cols_sb[:, 2, :], d_skip), (a_sb[:, :, :], a_log), (wo_sb[:, :, :], w_out),
            (wdt_sb[KP:KD, :], w_dt), (wx_sb[:, :, KP:KD], w_x[:, :, 0:RANK]),
        ] + [(wx_sb[:, :, r * NBC:(r + 1) * NBC], w_x[:, :, RANK:RANK + NBC]) for r in range(3)]
        n_weights = len(weight_loads)

        @block.sync
        def _(sp):
            def load(q):
                _, i, s = loads[q]
                old = q - RING
                if old >= 0:
                    if old in adds_at:
                        sp.wait_ge(adds_done, adds_at[old])
                    if old in blocks_at:
                        sp.wait_ge(blocks_done, blocks_at[old])
                    if old in pieces_at:
                        sp.wait_ge(lo_ready, pieces_at[old])
                    sp.wait_ge(ring_in[q % RING], 16 * (q // RING))
                sp.dma_start(ring[:, q % RING, :], adj[s, i]).then_inc(ring_in[q % RING], 16)

            for i in range(NS):
                for s in pass_a_order(i):
                    load(load_at["A", i, s])
                for b in range(BPS):
                    if i:
                        sp.wait_ge(adds_done, adds_per_strip * i)
                        sp.wait_ge(diag_done, i)
                        sp.wait_ge(diag_in[b], 16 * i)
                    sp.dma_start(diag[:, b, :], adj[BPS * i + b, i]).then_inc(diag_in[b], 16)
            first_c = load_at["C", 0, 0]
            for q in range(load_at["B", NS - 2, NB - 1], first_c):
                load(q)
            q = first_c
            for g in slots:
                pair = (g + 2) // 2
                if g % 2 == 0 and 0 <= pair < NCH * DS // 2:
                    k, n = divmod(2 * pair, DS)
                    sp.wait_ge(c_out, 16 * (k + 1))
                    if pair >= 2:
                        sp.wait_ge(mult_done, 2 * pair - 2)
                        sp.wait_ge(c_in[pair % 2], 16 * (pair // 2))
                    sp.dma_start(csb[pair % 2], c_dram[k:k + 1, n * T:(n + 2) * T].rearrange("a (n t) -> a n t", n=2)
                                 .to_broadcast([P, 2, T])).then_inc(c_in[pair % 2], 16)
                while q < len(loads) and block_end.get(q - RING, g) <= g:
                    load(q)
                    q += 1
            assert q == len(loads)

        @block.gpsimd
        def _(pool):
            nc.gpsimd.memset(ones[:, :], 1.0).then_inc(consts_done, 1)
            nc.gpsimd.memset(minus_half[:, :], -0.5).then_inc(consts_done, 1)
            nc.gpsimd.memset(state[:, :, :], 0.0).then_inc(consts_done, 1)

            def power(m, cols):
                pool.wait_ge(base_ready, m + 1)
                if m == 0:
                    pool.wait_ge(consts_done, 3)
                else:
                    pool.wait_ge(norm_ready, m)
                nc.gpsimd.tensor_tensor(rstd[:, 0:cols], base[:, 0:cols], minus_half[:, 0:cols],
                                        ALU.pow).then_inc(pow_done, 1)

            for m in range(3 * NS):
                power(m, TPS)

            for g in range(FIRST_SLOT, LAST_SLOT):
                k, n = divmod(g, DS)
                if n == 4 and 0 <= k + 1 < NCH:
                    power(3 * NS + k + 1, CT)
                if 0 <= k < NCH:
                    buf = hs[g % HSB]
                    pool.wait_ge(scan_done, 2 * (g + 1))
                    nc.gpsimd.tensor_copy(state[:, :, n:n + 1], buf[:, :, T - 1:T]).then_inc(state_saved, 1)
                    pool.wait_ge(state_saved, g + 1)
                    pool.wait_ge(c_in[g // 2 % 2], 16 * (g // 4 + 1))
                    nc.gpsimd.tensor_tensor(buf, buf, csb[g // 2 % 2][:, g % 2:g % 2 + 1, :].to_broadcast([P, HALVES, T]),
                                            ALU.mult).then_inc(mult_done, 1)
                    if n % 2:
                        pool.wait_ge(mult_done, g + 1)
                        even = hs[(g - 1) % HSB]
                        nc.gpsimd.tensor_tensor(even, even, buf, ALU.add).then_inc(pair_done, 1)

        @block.vector
        def _(dve):
            steps = [0]

            def step(ins):
                steps[0] += 1
                ins.then_inc(dve_step, 1)
                dve.wait_ge(dve_step, steps[0])

            powers = [0]

            def norm_stats(tiles):
                n = len(tiles)
                for t, v in enumerate(tiles):
                    ins = nc.vector.bn_stats(stats[:, t, :], v)
                step(ins)
                for t in range(n):
                    ins = nc.vector.bn_aggr(mv[:, t, :], stats[:, t, :])
                step(ins)
                powers[0] += 1
                nc.vector.tensor_scalar(base[:, 0:n], mv[:, 0:n, 1], LN_EPS, None, ALU.add).then_inc(base_ready, 1)

            def norm_bias(n):
                dve.wait_ge(pow_done, powers[0])
                nc.vector.scalar_tensor_tensor(nmr[:, 0:n], mv[:, 0:n, 0], -1.0, rstd[:, 0:n],
                                               ALU.mult, ALU.mult).then_inc(norm_ready, 1)

            dve.wait_ge(weights_in, 16 * n_weights)
            dve.wait_ge(consts_done, 3)
            for r in range(3):
                step(nc.vector.tensor_copy(pick[r * NBC:(r + 1) * NBC, :],
                                           ident[r * NBC:(r + 1) * NBC, r * NBC:(r + 1) * NBC]))
            dve.wait_ge(a_done, 1)
            step(nc.vector.tensor_scalar(a_sb[:, :, :], a_sb[:, :, :], -1.0, None, ALU.mult))
            total_adds = 0
            rowacc_blocks = rowacc
            for i in range(NS):
                order = [("ring", load_at["A", i, s]) for s in pass_a_order(i)] + [("diag", b) for b in range(BPS)]

                def arrived(where):
                    kind, q = where
                    if kind == "ring":
                        dve.wait_ge(ring_in[q % RING], 16 * (q // RING + 1))
                        return ring[:, q % RING, :]
                    dve.wait_ge(diag_in[q], 16 * (i + 1))
                    return diag[:, q, :]

                dve.wait_ge(xs_in[i % 2], 16 * (i // 2 + 1))
                if i:
                    dve.wait_ge(normed, i)
                norm_stats([tile_of(xs[i % 2], t) for t in range(TPS)])
                norm_bias(TPS)
                if i:
                    dve.wait_ge(fold_done, i)
                first, second = arrived(order[0]), arrived(order[1])
                total_adds += 1
                nc.vector.tensor_tensor(rowacc_blocks, first, second, ALU.add).then_inc(adds_done, 1)
                for where in order[2:]:
                    v = arrived(where)
                    dve.wait_ge(adds_done, total_adds)
                    total_adds += 1
                    nc.vector.tensor_tensor(rowacc_blocks, rowacc_blocks, v, ALU.add).then_inc(adds_done, 1)
                dve.wait_ge(fold_done, i + 1)
                dve.wait_ge(normed, i + 1)
                powers[0] += 1
                nc.vector.tensor_scalar(base[:, :], ps_deg, DEG_EPS, None, ALU.add).then_inc(base_ready, 1)
                dve.wait_ge(pow_done, powers[0])
                deg = dcol[:, i * TPS:(i + 1) * TPS]
                nc.vector.tensor_copy(deg, rstd[:, :]).then_inc(norm_ready, 1)
                dve.wait_ge(norm_ready, powers[0])
                hv = rows(h0[:, i * STRIP:(i + 1) * STRIP], TPS)
                nc.vector.tensor_tensor(hv, hv, deg.unsqueeze(2).to_broadcast([P, TPS, F]),
                                        ALU.mult).then_inc(h0_ready, 1)

            def low_part(r, q, a):
                buf, blk = r % 2, r // JT
                if a == 0:
                    s = loads[q][2]
                    dve.wait_ge(h_hi_ready, 2 * (blk + 1))
                    for layer, h in enumerate((h0, h1)):
                        nc.vector.tensor_tensor(h_parts[:, blk % 2, layer, 1, :],
                                                h[:, JT * s * F:JT * (s + 1) * F],
                                                h_parts[:, blk % 2, layer, 0, :].bitcast(F32), ALU.subtract)\
                            .then_inc(h_lo_ready, 1)
                dve.wait_ge(hi_ready, r + 1)
                nc.vector.tensor_tensor(adj_parts[:, buf, 1, :], ring[:, q % RING, a * STRIP:(a + 1) * STRIP],
                                        adj_parts[:, buf, 0, :].bitcast(F32), ALU.subtract).then_inc(lo_ready, 1)

            def complete(n, stage):
                i = NS - 1 - n
                if stage == 0 and n:
                    dve.wait_ge(layer0_sum, n)
                    dve.wait_ge(l0_back[n % 2], 16 * (n // 2 + 1))
                    dve.wait_ge(w_done, n)
                    nc.vector.tensor_tensor(halves(s0), acc0[i % 2], halves(l0_sums[n % 2]), ALU.add)\
                        .then_inc(s0_ready, 1)
                if stage == 1:
                    dve.wait_ge(w_done, n + 1)
                    deg = dcol[:, i * TPS:(i + 1) * TPS].unsqueeze(2).to_broadcast([P, TPS, F])
                    pv = rows(pre, TPS)
                    step(nc.vector.tensor_tensor(pv, ps_w.rearrange("p b (t f) -> p (b t) f", f=F), deg, ALU.mult))
                    step(nc.vector.tensor_tensor(pv, pv, b0_sb[:, :].unsqueeze(1).to_broadcast([P, TPS, F]),
                                                 ALU.add))
                    dve.wait_ge(xs_in[n % 2], 16 * (NS // 2 + n // 2 + 1))
                    if n >= 2:
                        dve.wait_ge(x1_out[n % 2], 16 * (n // 2))
                    if n:
                        dve.wait_ge(normed, NS + n)
                    nc.vector.scalar_tensor_tensor(x1[n % 2], pre, 0.0, xs[n % 2], ALU.max, ALU.add)\
                        .then_inc(x1_ready, 1)
                    dve.wait_ge(x1_ready, n + 1)
                if stage == 3:
                    norm_stats([tile_of(x1[n % 2], t) for t in range(TPS)])
                if stage == 4:
                    norm_bias(TPS)

            for stage in range(5):
                complete(0, stage)
            r = 0
            for n, i in enumerate(reversed(range(NS - 1))):
                strip_pieces = [(load_at["B", i, s], a) for s in reversed(range(BPS * (i + 1), NB)) for a in range(JT)]
                for m, (q, a) in enumerate(strip_pieces):
                    if r >= 2:
                        dve.wait_ge(pieces_done, r - 1)
                    low_part(r, q, a)
                    r += 1
                    if n:
                        complete(n, m)
            for stage in range(5):
                complete(NS - 1, stage)

            for g in range(FIRST_SLOT, LAST_SLOT):
                k, n = divmod(g, DS)
                pk, qk = k + 1, k - 1
                for i in range(NS):
                    if handover[i] != g:
                        continue
                    dve.wait_ge(blocks_done, blocks_at[load_at["C", i, BPS * (i + 1) - 1]])
                    if i < NS - 1:
                        dve.wait_ge(l1_back[i % 2], 16 * (i // 2 + 1))
                        nc.vector.tensor_tensor(halves(s1[i % 2]), acc_c, halves(s1[i % 2]), ALU.add)\
                            .then_inc(s1_ready, 1)
                    else:
                        dve.wait_ge(misc_full, misc_at["gcn", CPS * (i - 1) - 1] + 1)
                        nc.vector.tensor_copy(halves(s1[i % 2]), acc_c).then_inc(s1_ready, 1)
                if 0 <= k < NCH:
                    if n == 0:
                        dve.wait_ge(dt_ready, 2 * (k + 1))
                    dve.wait_ge(b_ready, g + 1)
                    if g:
                        dve.wait_ge(scan_done, 2 * g)
                    nc.vector.tensor_tensor(dbu, w[k % 2], b_ps[g % 2].unsqueeze(1).to_broadcast([P, HALVES, T]),
                                            ALU.mult).then_inc(dbu_done, 1)
                    dve.wait_ge(dbu_done, g + 1)
                    dve.wait_ge(da_ready, g + 1)
                    if k:
                        dve.wait_ge(state_saved, g - DS + 1)
                    if g // 2 >= HSB // 2:
                        dve.wait_ge(nsum_done, g // 2 - HSB // 2 + 1)
                    for h in range(HALVES):
                        nc.vector.tensor_tensor_scan(hs[g % HSB][:, h, :], da[g % 2][:, h, :], dbu[:, h, :],
                                                     state[:, h, n:n + 1], ALU.mult, ALU.add).then_inc(scan_done, 1)
                if n == 3 and 0 <= qk < NCH:
                    dve.wait_ge(nsum_done, DS // 2 * (qk + 1))
                    if qk:
                        dve.wait_ge(misc_full, misc_at["out", qk - 1] + 1)
                    for h in range(HALVES):
                        ins = nc.vector.scalar_tensor_tensor(yg[:, h, :], u[qk % 2][:, h, :], cols_sb[:, 2, h:h + 1],
                                                             y_ps[:, h, :], ALU.mult, ALU.add)
                    ins.then_inc(y_free, 1)
                    dve.wait_ge(y_free, qk + 1)
                    nc.vector.tensor_tensor(yg, yg, sz[qk % 2], ALU.mult).then_inc(yg_ready, 1)
                if n == 4 and pk < NCH:
                    dve.wait_ge(misc_full, misc_at["gcn", pk] + 1)
                    if pk:
                        dve.wait_ge(misc_full, misc_at["tr", pk - 1] + 1)
                    nc.vector.tensor_tensor(gbuf, rows(misc_of("gcn", pk), CT),
                                            gb_sb[:, :].unsqueeze(1).to_broadcast([P, CT, F]), ALU.add)\
                        .then_inc(misc_free[misc_at["gcn", pk] % 2], 1)
                    evacuated(dve, "gcn", pk)
                    step(nc.vector.tensor_scalar(gbuf, gbuf, 0.0, None, ALU.max))
                    dve.wait_ge(normed, NORM_C + pk)
                    norm_stats([gbuf[:, t, :] for t in range(CT)])
                if n == 5 and pk < NCH:
                    norm_bias(CT)
                if n == 5 and 0 <= qk < NCH:
                    dve.wait_ge(misc_full, misc_at["out", qk] + 1)
                    dve.wait_ge(x1t_in[qk % 2], 16 * (qk // 2 + 1))
                    nc.vector.tensor_tensor(x1t[qk % 2], rows(misc_of("out", qk), CT), x1t[qk % 2], ALU.add)\
                        .then_inc(misc_free[misc_at["out", qk] % 2], 1)
                if n in (8, 9) and pk < NCH:
                    h = n - 8
                    xc = xcp[pk % 2][:, h, :]
                    if pk:
                        ins = nc.vector.tensor_copy(xc[:, 1:CONV], xcp[(pk - 1) % 2][:, h, T + 1:T + CONV])
                    else:
                        ins = nc.vector.memset(xc[:, 1:CONV], 0.0)
                    step(ins)
                    evacuated(dve, f"xz{h}", pk)
                    acc = cv[:, h, :]
                    step(nc.vector.tensor_scalar(acc, xc[:, 1:1 + T], conv_sb[:, h, 0:1], cols_sb[:, 0, h:h + 1],
                                                 ALU.mult, ALU.add))
                    for tap in range(1, CONV):
                        ins = nc.vector.scalar_tensor_tensor(acc, xc[:, 1 + tap:1 + tap + T],
                                                             conv_sb[:, h, tap:tap + 1], acc, ALU.mult, ALU.add)
                        if tap < CONV - 1:
                            step(ins)
                    ins.then_inc(conv_done, 1)
                if n == 12 and pk < NCH:
                    pb = parts[pk % 2]
                    evacuated(dve, "dbc", pk)
                    step(nc.vector.tensor_copy(pb[:, :], bcv[0:KP, :]))
                    dve.wait_ge(c_out, 16 * (pk + 1))
                    step(nc.vector.tensor_tensor(bcv[0:KP, :], bcv[0:KP, :], pb[:, :], ALU.subtract))
                    for r in (1, 2):
                        ins = nc.vector.tensor_copy(pb[r * NBC:(r + 1) * NBC, :], bcv[r * NBC:(r + 1) * NBC, :])
                    step(ins)
                    third = slice(2 * NBC, 3 * NBC)
                    step(nc.vector.tensor_tensor(bcv[third, :], bcv[third, :], pb[third, :], ALU.subtract))
                    nc.vector.tensor_copy(pb[third, :], bcv[third, :]).then_inc(parts_ready, 1)
                ex, w1 = w[pk % 2], dt[pk % 2]
                if n == 13 and pk < NCH:
                    dve.wait_ge(ex_ready, pk + 1)
                    step(nc.vector.tensor_scalar(w1, ex, 1.0, None, ALU.add))
                    nc.vector.scalar_tensor_tensor(ex, w1, -1.0, ex, ALU.add, ALU.subtract).then_inc(w1_ready, 1)
                    dve.wait_ge(w1_ready, pk + 1)
                    step(nc.vector.scalar_tensor_tensor(ex, cv, 0.0, ex, ALU.max, ALU.subtract))
                if n == 14 and pk < NCH:
                    dve.wait_ge(log_ready, pk + 1)
                    nc.vector.tensor_tensor(dt[pk % 2], ex, w1, ALU.add).then_inc(dt_ready, 1)
                    dve.wait_ge(dt_ready, 2 * pk + 1)
                    dve.wait_ge(u_ready, pk + 1)
                    nc.vector.tensor_tensor(w[pk % 2], dt[pk % 2], u[pk % 2], ALU.mult).then_inc(dt_ready, 1)

        @block.tensor
        def _(pe):
            def arrived(q):
                pe.wait_ge(ring_in[q % RING], 16 * (q // RING + 1))
                return ring[:, q % RING, :]

            def product(acc, h, s, blk, start, stop, todo=None):
                for a in range(JT):
                    for c in range(STRIP // MM):
                        last = nc.tensor.matmul(acc[:, c, :], tile_of(h, JT * s + a),
                                                blk[:, a * STRIP + c * MM:a * STRIP + (c + 1) * MM],
                                                start=start and a == 0, stop=stop and a == JT - 1)
                return last

            pe.wait_ge(consts_done, 3)
            def diagonal(i):
                pe.wait_ge(h0_ready, i + 1)
                for b in range(BPS):
                    pe.wait_ge(diag_in[b], 16 * (i + 1))
                    last = product(acc0[i % 2], h0, BPS * i + b, diag[:, b, :], i == 0 and b == 0, b == BPS - 1)
                last.then_inc(diag_done, 1)

            for i in range(NS):
                lower = [s for s in pass_a_order(i) if s < BPS * i]
                if i >= 2:
                    pe.wait_ge(part_ready, i - 1)
                for n, s in enumerate(lower):
                    if n == min(AHEAD, len(lower) - BPS):
                        diagonal(i - 1)
                    pe.wait_ge(h0_ready, s // BPS + 1)
                    product(acc0[i % 2], h0, s, arrived(load_at["A", i, s]), n == 0, False)\
                        .then_inc(blocks_done, 1)
                pe.wait_ge(adds_done, adds_per_strip * (i + 1))
                if i:
                    pe.wait_ge(h0_ready, i)
                for t in range(TPS):
                    for a in range(JT):
                        last = nc.tensor.matmul(ps_deg[:, t:t + 1],
                                                rowacc[:, a * STRIP + t * P:a * STRIP + (t + 1) * P], ones[:, :],
                                                start=a == 0, stop=a == JT - 1)
                last.then_inc(fold_done, 1)
            diagonal(NS - 1)

            def through_w(n, i):
                if n == 0:
                    pe.wait_ge(l0_back[0], 16)
                    src = l0_sums[0]
                else:
                    pe.wait_ge(s0_ready, n)
                    pe.wait_ge(x1_ready, n)
                    src = s0
                for t in range(TPS):
                    last = nc.tensor.matmul(ps_w[:, t // CT, t % CT * F:(t % CT + 1) * F],
                                            src[:, t * P:(t + 1) * P], w0t_sb[:, :], start=True, stop=True)
                last.then_inc(w_done, 1)

            pe.wait_ge(weights_in, 16 * n_weights)
            through_w(0, NS - 1)
            def split_product(acc, r, a, layer, start, stop):
                buf, blk = r % 2, r // JT
                for adj_part, h_part in ((0, 0), (0, 1), (1, 0)):
                    if adj_part:
                        pe.wait_ge(lo_ready, r + 1)
                    for c in range(STRIP // MM):
                        last = nc.tensor.matmul(
                            acc[:, c, :], h_parts[:, blk % 2, layer, h_part, a * F:(a + 1) * F],
                            adj_parts[:, buf, adj_part, c * MM:(c + 1) * MM],
                            start=start and (adj_part, h_part) == (0, 0), stop=stop and adj_part == 1)
                return last

            r = 0
            for n, i in enumerate(reversed(range(NS - 1))):
                strip_pieces = [(s, a) for s in reversed(range(BPS * (i + 1), NB)) for a in range(JT)]
                if n < 2:
                    pe.wait_ge(part_ready, NS)
                else:
                    pe.wait_ge(s0_ready, n - 1)
                for m, (s, a) in enumerate(strip_pieces):
                    start, stop = m == 0, m == len(strip_pieces) - 1
                    pe.wait_ge(hi_ready, r + 1)
                    pe.wait_ge(h_lo_ready, 2 * (r // JT + 1))
                    last = split_product(acc0[i % 2], r, a, 0, start, stop)
                    if stop:
                        last.then_inc(layer0_sum, 1)
                    if start and n:
                        pe.wait_ge(l1_staged, n)
                    split_product(acc1, r, a, 1, start, stop).then_inc(pieces_done, 1)
                    r += 1
                    if m == 0 and n:
                        through_w(n, i + 1)
            through_w(NS - 1, 0)

            def c_products(mms):
                for i, s, a, c in mms:
                    q = load_at["C", i, s]
                    blk = arrived(q) if (a, c) == (0, 0) else ring[:, q % RING, :]
                    if (s, a, c) == (0, 0, 0):
                        pe.wait_ge(normed, NORM_C)
                        if i:
                            pe.wait_ge(s1_ready, i)
                    last = nc.tensor.matmul(acc_c[:, c, :], tile_of(h1, JT * s + a),
                                            blk[:, a * STRIP + c * MM:a * STRIP + (c + 1) * MM],
                                            start=s == 0 and a == 0, stop=s == BPS * (i + 1) - 1 and a == JT - 1)
                    if (a, c) == (JT - 1, STRIP // MM - 1):
                        last.then_inc(blocks_done, 1)

            def use_misc(key):
                m = misc_at[key]
                if m >= 2:
                    pe.wait_ge(misc_free[m % 2], m // 2)
                return misc_ps[m % 2]

            c_products(products[FIRST_SLOT - 1])
            for g in range(FIRST_SLOT, LAST_SLOT):
                k, n = divmod(g, DS)
                pk, qk = k + 1, k - 1
                if 0 <= g + 1 < NCH * DS:
                    kk, nn = divmod(g + 1, DS)
                    pe.wait_ge(parts_ready, kk + 1)
                    if g + 1 >= 2:
                        pe.wait_ge(dbu_done, g)
                    pv = parts[kk % 2]
                    nc.tensor.matmul(b_ps[(g + 1) % 2], pick[:, nn:nn + 1].to_broadcast([KP, P]), pv[:, :],
                                     start=True, stop=True).then_inc(b_ready, 1)
                G, odd = divmod(g - 4, 2)
                if not odd and 0 <= G < NCH * DS // 2:
                    pe.wait_ge(pair_done, G + 1)
                    first = G % (DS // 2) == 0
                    if first and G:
                        pe.wait_ge(y_free, G // (DS // 2))
                    if G == 0:
                        pe.wait_ge(normed, NORM_C)
                    for h in range(HALVES):
                        last = nc.tensor.matmul(y_ps[:, h, :], ident[:, :], hs[2 * G % HSB][:, h, :],
                                                start=first, stop=G % (DS // 2) == DS // 2 - 1)
                    last.then_inc(nsum_done, 1)
                if pk < NCH:
                    if n == 3:
                        pe.wait_ge(s1_ready, pk // CPS + 1)
                        m_ps = use_misc(("gcn", pk))
                        for t in range(CT):
                            c = pk % CPS * T + t * P
                            last = nc.tensor.matmul(m_ps[:, t * F:(t + 1) * F], s1[pk // CPS % 2][:, c:c + P], gw_sb[:, :],
                                                    start=True, stop=True)
                        last.then_inc(misc_full, 1)
                if n == 5 and 0 <= qk < NCH:
                    pe.wait_ge(yg_ready, qk + 1)
                    m_ps = use_misc(("out", qk))
                    for t in range(CT):
                        for h in range(HALVES):
                            last = nc.tensor.matmul(m_ps[:, t * F:(t + 1) * F], yg[:, h, t * P:(t + 1) * P],
                                                    wo_sb[:, h, :], start=h == 0, stop=h == HALVES - 1)
                    last.then_inc(misc_full, 1)
                if pk < NCH:
                    if n == 6:
                        pe.wait_ge(normed, NORM_C + pk + 1)
                        m_ps = use_misc(("tr", pk))
                        for t in range(CT):
                            last = nc.tensor.transpose(m_ps[:, t * P:(t + 1) * P], gbuf[:, t, :], ident[:, :])
                        last.then_inc(misc_full, 1)
                    if 7 <= n <= 10:
                        c = n - 7
                        evacuated(pe, "tr", pk)
                        m_ps = use_misc((f"xz{c}", pk))
                        nc.tensor.matmul(m_ps, w_in_sb[:, c * P:(c + 1) * P], h_t, start=True, stop=True)\
                            .then_inc(misc_full, 1)
                    if n == 11:
                        pe.wait_ge(u_ready, pk + 1)
                        m_ps = use_misc(("dbc", pk))
                        for h in range(HALVES):
                            last = nc.tensor.matmul(m_ps[0:KD, :], wx_sb[:, h, :], u[pk % 2][:, h, :],
                                                    start=h == 0, stop=h == HALVES - 1)
                        last.then_inc(misc_full, 1)
                    if n == 12:
                        for h in range(HALVES):
                            evacuated(pe, "dbc", pk)
                            m_ps = use_misc((f"dt{h}", pk))
                            nc.tensor.matmul(m_ps, wdt_sb[KP:KD, h * P:(h + 1) * P], bcv[KP:KD, :],
                                             start=True, stop=True).then_inc(misc_full, 1)
                c_products(products[g])

        @block.scalar
        def _(act):
            for dst, src in weight_loads:
                act.dma_start(dst, src).then_inc(weights_in, 16)

            def load_xs(n, i):
                act.dma_start(xs[n % 2], x[:, i * STRIP:(i + 1) * STRIP]).then_inc(xs_in[n % 2], 16)

            def normalise(src, dst, n, func):
                for t in range(n):
                    last = nc.scalar.activation(dst[t], src[t], func, bias=nmr[:, t:t + 1], scale=rstd[:, t:t + 1])
                last.then_inc(normed, 1)

            load_xs(0, 0)
            load_xs(1, 1)
            act.wait_ge(weights_in, 16 * n_weights)
            nc.scalar.activation(a_sb[:, :, :], a_sb[:, :, :], ACT.Exp).then_inc(a_done, 1)

            def move_part(i):
                act.wait_ge(diag_done, i + 1)
                if i >= 2:
                    act.wait_ge(l0_out[i % 2], 16 * (i // 2))
                nc.scalar.activation(halves(l0_sums[i % 2]), acc0[i % 2], ACT.Copy).then_inc(part_ready, 1)
                act.wait_ge(part_ready, i + 1)
                act.dma_start(lower0_dram[:, i * STRIP:(i + 1) * STRIP], l0_sums[i % 2]).then_inc(l0_out[i % 2], 16)

            for i in range(NS):
                act.wait_ge(norm_ready, 2 * i + 1)
                normalise([tile_of(xs[i % 2], t) for t in range(TPS)],
                          [tile_of(h0, i * TPS + t) for t in range(TPS)], TPS, ACT.Relu)
                act.wait_ge(normed, i + 1)
                m = i + 2
                load_xs(m, m if m < NS else 2 * NS - 1 - m)
                if i:
                    move_part(i - 1)
            move_part(NS - 1)

            def load_l0(n):
                i = NS - 1 - n
                act.dma_start(l0_sums[n % 2], lower0_dram[:, i * STRIP:(i + 1) * STRIP]).then_inc(l0_back[n % 2], 16)

            for b in range(2):
                act.wait_ge(l0_out[b], 16 * NS // 2)
            for n in range(2):
                load_l0(n)

            def high_part(r, q, a):
                buf, blk = r % 2, r // JT
                if r >= 2:
                    act.wait_ge(pieces_done, r - 1)
                if a == 0:
                    s = loads[q][2]
                    for layer, h in enumerate((h0, h1)):
                        if layer:
                            act.wait_ge(normed, NS + NS - s // BPS)
                        nc.scalar.activation(h_parts[:, blk % 2, layer, 0, :], h[:, JT * s * F:JT * (s + 1) * F],
                                             ACT.Copy).then_inc(h_hi_ready, 1)
                    act.wait_ge(ring_in[q % RING], 16 * (q // RING + 1))
                nc.scalar.activation(adj_parts[:, buf, 0, :], ring[:, q % RING, a * STRIP:(a + 1) * STRIP],
                                     ACT.Copy).then_inc(hi_ready, 1)

            def layer1_input(n):
                i = NS - 1 - n
                act.wait_ge(norm_ready, 2 * NS + n + 1)
                if n == 0:
                    act.wait_ge(diag_done, NS)
                normalise([tile_of(x1[n % 2], t) for t in range(TPS)],
                          [tile_of(h1, i * TPS + t) for t in range(TPS)], TPS, ACT.Relu)
                act.dma_start(x1_dram[:, i * STRIP:(i + 1) * STRIP], x1[n % 2]).then_inc(x1_out[n % 2], 16)
                m = n + 2
                if m < NS:
                    load_xs(m, NS - 1 - m)
                    if n:
                        act.wait_ge(s0_ready, n)
                    else:
                        act.wait_ge(w_done, 1)
                    load_l0(m)

            def move_layer1(n, i):
                act.wait_ge(pieces_done, pieces_at[load_at["B", i, BPS * (i + 1)]])
                if n:
                    act.wait_ge(l1_out, 16 * n)
                nc.scalar.activation(halves(l1_stage), acc1, ACT.Copy).then_inc(l1_staged, 1)
                act.wait_ge(l1_staged, n + 1)
                act.dma_start(upper1_dram[:, i * STRIP:(i + 1) * STRIP], l1_stage).then_inc(l1_out, 16)

            layer1_input(0)
            r = 0
            for n, i in enumerate(reversed(range(NS - 1))):
                strip_pieces = [(load_at["B", i, s], a) for s in reversed(range(BPS * (i + 1), NB)) for a in range(JT)]
                for m, (q, a) in enumerate(strip_pieces):
                    high_part(r, q, a)
                    r += 1
                    if n and m == 0:
                        move_layer1(n - 1, i + 1)
                    if n and m == 5:
                        layer1_input(n)
            move_layer1(NS - 2, 0)
            layer1_input(NS - 1)

            def load_x1t(k):
                act.dma_start(x1t[k % 2], rows(x1_dram[:, k * T:(k + 1) * T], CT)).then_inc(x1t_in[k % 2], 16)

            for b in range(2):
                act.wait_ge(x1_out[b], 16 * NS // 2)
            act.wait_ge(l1_out, 16 * (NS - 1))
            act.wait_ge(w_done, NS)
            act.wait_ge(normed, NORM_C)
            for g in range(FIRST_SLOT, LAST_SLOT):
                k, n = divmod(g, DS)
                pk, qk = k + 1, k - 1
                if 0 <= g + 1 < NCH * DS:
                    kk, nn = divmod(g + 1, DS)
                    if nn == 0:
                        act.wait_ge(dt_ready, 2 * kk + 1)
                    if g + 1 >= 2:
                        act.wait_ge(scan_done, 2 * g)
                    for h in range(HALVES):
                        last = nc.scalar.activation(da[(g + 1) % 2][:, h, :], dt[kk % 2][:, h, :], ACT.Exp,
                                                    scale=a_sb[:, h, nn:nn + 1])
                    last.then_inc(da_ready, 1)
                for i in range(NS - 1):
                    if max(handover[i] - 2, FIRST_SLOT) == g:
                        if i >= 2:
                            act.wait_ge(misc_full, misc_at["gcn", CPS * (i - 1) - 1] + 1)
                        act.dma_start(s1[i % 2], upper1_dram[:, i * STRIP:(i + 1) * STRIP])\
                            .then_inc(l1_back[i % 2], 16)
                if n == 1 and 0 <= k < NCH:
                    if k >= 2:
                        act.wait_ge(out_done[k % 2], 16 * (k // 2))
                    load_x1t(k)
                ex, w1 = w[pk % 2], dt[pk % 2]
                if pk < NCH:
                    def evacuate(key, dst, **more):
                        act.wait_ge(misc_full, misc_at[key] + 1)
                        src = misc_of(*key)[0:dst.shape[0], :]
                        nc.scalar.activation(dst, src, ACT.Identity if more else ACT.Copy, **more)\
                            .then_inc(misc_free[misc_at[key] % 2], 1)

                    if n == 5:
                        act.wait_ge(norm_ready, 3 * NS + pk + 1)
                        g4 = [gbuf[:, t, :] for t in range(CT)]
                        normalise(g4, g4, CT, ACT.Identity)
                    if n == 6:
                        evacuate(("tr", pk), h_t, scale=ln_sb[:, 0:1], bias=ln_sb[:, 1:2])
                    if n in (7, 8):
                        if pk >= 2:
                            act.wait_ge(conv_done, HALVES * pk)
                        evacuate((f"xz{n - 7}", pk), xcp[pk % 2][:, n - 7, CONV:CONV + T])
                    if n in (9, 10):
                        if pk >= 2:
                            act.wait_ge(yg_ready, pk - 1)
                        evacuate((f"xz{n - 7}", pk), sz[pk % 2][:, n - 9, :])
                    if n == 10:
                        act.wait_ge(conv_done, HALVES * (pk + 1))
                        nc.scalar.activation(u[pk % 2], cv, ACT.Silu).then_inc(u_ready, 1)
                        evacuated(act, "xz3", pk)
                        nc.scalar.activation(sz[pk % 2], sz[pk % 2], ACT.Silu).then_inc(sz_ready, 1)
                    if n == 11:
                        evacuate(("dbc", pk), bcv[0:KD, :])
                        evacuated(act, "dbc", pk)
                        act.dma_start(c_dram[pk:pk + 1, :].rearrange("a (n t) -> (a n) t", n=DS), bcv[DS:2 * DS, :])\
                            .then_inc(c_out, 16)
                    if n == 12:
                        for h in range(HALVES):
                            evacuate((f"dt{h}", pk), cv[:, h, :], bias=cols_sb[:, 1, h:h + 1],
                                     scale=1.0)
                        evacuated(act, "dt1", pk)
                        nc.scalar.activation(ex, cv, ACT.Abs).then_inc(act_step, 1)
                        act.wait_ge(act_step, pk + 1)
                        nc.scalar.activation(ex, ex, ACT.Exp, scale=-1.0).then_inc(ex_ready, 1)
                    if n == 13:
                        act.wait_ge(w1_ready, pk + 1)
                        nc.scalar.activation(w1, w1, ACT.Ln).then_inc(log_ready, 1)
                if n == 6 and 0 <= qk < NCH:
                    evacuated(act, "out", qk)
                    act.dma_start(rows(out[:, qk * T:(qk + 1) * T], CT), x1t[qk % 2]).then_inc(out_done[qk % 2], 16)
            for b in range(2):
                act.wait_ge(out_done[b], 16 * NCH // 2)


def kernel(x, adj, L0_gnn_W, L0_gnn_b, L1_gnn_gcn_w, L1_gnn_gcn_b, L1_gnn_ln_g, L1_gnn_ln_b, L1_gnn_w_in,
           L1_gnn_conv_w, L1_gnn_conv_b, L1_gnn_w_xp, L1_gnn_w_dt, L1_gnn_b_dt, L1_gnn_A_log, L1_gnn_D_skip,
           L1_gnn_w_out):
    import numpy as np
    import concourse.bacc as bacc
    from concourse.bass_utils import run_bass_kernel_spmd

    def by_halves(a):
        a = np.asarray(a)
        return a.reshape(HALVES, P, -1).transpose(1, 0, 2)

    def column(a):
        return np.asarray(a).reshape(P, 1)

    laid_out = {
        "adj": np.asarray(adj).reshape(NS, STRIP, NB, JT, P).transpose(2, 0, 4, 3, 1).reshape(NB, NS, P, BLOCK),
        "x": np.asarray(x).reshape(N // P, P, F).transpose(1, 0, 2).reshape(P, N),
        "w0t": np.asarray(L0_gnn_W).T,
        "b0": np.asarray(L0_gnn_b).reshape(1, F),
        "gcn_w": L1_gnn_gcn_w,
        "gcn_b": np.asarray(L1_gnn_gcn_b).reshape(1, F),
        "ln_g": column(L1_gnn_ln_g),
        "ln_b": column(L1_gnn_ln_b),
        "w_in": L1_gnn_w_in,
        "conv_w": by_halves(L1_gnn_conv_w),
        "conv_b": by_halves(L1_gnn_conv_b)[:, :, 0],
        "w_x": by_halves(L1_gnn_w_xp),
        "w_dt": L1_gnn_w_dt,
        "b_dt": by_halves(L1_gnn_b_dt)[:, :, 0],
        "a_log": by_halves(L1_gnn_A_log),
        "d_skip": by_halves(L1_gnn_D_skip)[:, :, 0],
        "w_out": by_halves(L1_gnn_w_out),
        "ident_in": np.eye(P, dtype=np.float32),
    }
    nc = bacc.Bacc("TRN2", target_bir_lowering=False, num_devices=1)
    arrays, args = {}, {}
    for name, a in laid_out.items():
        arrays[name] = np.ascontiguousarray(a)
        args[name] = nc.dram_tensor(name, arrays[name].shape, F32, kind="ExternalInput").ap()
    out = nc.dram_tensor("out", (P, N), F32, kind="ExternalOutput").ap()
    build(nc, out=out, **args)
    got = run_bass_kernel_spmd(nc, [arrays], core_ids=[0]).results[0]["out"]
    return np.ascontiguousarray(got.reshape(P, N // P, F).transpose(1, 0, 2).reshape(N, F))
```

```python
from contextlib import ExitStack

import concourse.bass as bass
from concourse import mybir

P = 128
N = 8192
F = 128
DI = 256
DS = 16
RANK = 8
HALVES = DI // P
STRIP = 1024
NS = N // STRIP
TPS = STRIP // P
BJ = 256
JT = BJ // P
NB = N // BJ
BPS = STRIP // BJ
BLOCK = JT * STRIP
MM = 512
RING = 7
RING_C = 6
T = 512
NCH = N // T
ARENA = 26 * STRIP + 8
CPS = STRIP // T
CT = T // P
NBC = 2 * DS
RANKS = NBC
LOW = 2 * NBC
KP = LOW + NBC
KD = KP + RANK
CONV = 4
LN_EPS = 1e-5
DEG_EPS = 1e-9
HSB = 8
AHEAD = 12
KEPT = 1
GCN, BIAS, STATS, POWER, NORMALISE, HALO = -19, -19, -17, -17, -15, -17
TRANSPOSE, XZ, CONVOLVE, SILU, DBC, SPLIT = -13, -12, (-10, -9, -8), -7, -6, -5
DT, SOFTPLUS, TIME_STEP, WEIGHTED_U = -4, -3, -2, -1
NSUM = 6
LOAD_X1, SKIP, GATE, OUT, RESIDUAL = 12, 20, 21, 25, 25
QUADS = (1, 3)
QUAD = 6
SPARED = 3

F32 = mybir.dt.float32
F32R = mybir.dt.float32r
ALU = mybir.AluOpType
ACT = mybir.ActivationFunctionType


def pass_a_order(i):
    lower, upper = list(range(BPS * i)), list(range(BPS * (i + 1), NB))
    total, products = len(lower) + len(upper), len(lower)
    return [(lower if (n + 1) * products // total > n * products // total else upper).pop(0) for n in range(total)]


def chunk_at(g, stage):
    k, n = divmod(g - stage, DS)
    return k if n == 0 and 0 <= k < NCH else None


def build(nc, adj, x, w0t, b0, gcn_w, gcn_b, ln_g, ln_b, w_in, conv_w, conv_b, w_x, w_dt, b_dt, a_log, d_skip,
          w_out, ident_in, out):
    x1_dram = nc.dram_tensor("x1_scratch", (P, N // P * F), F32, kind="Internal").ap()
    lower0_dram = nc.dram_tensor("lower0_scratch", (P, N), F32, kind="Internal").ap()
    c_dram = nc.dram_tensor("c_scratch", (NCH, DS * T), F32, kind="Internal").ap()
    upper1_dram = nc.dram_tensor("upper1_scratch", (P, N), F32, kind="Internal").ap()

    loads = [("A", i, s) for i in range(NS) for s in pass_a_order(i)]
    loads += [("B", i, s) for i in reversed(range(NS)) for s in reversed(range(BPS * (i + 1), NB))]
    rows_of = {i: list(range(BPS * (i + 1))) for i in range(NS)}
    rows_of[1] = rows_of[1][BPS:] + rows_of[1][:BPS]
    loads += [("C", 1, s) for s in rows_of[1][:BPS]] + [("C", 0, s) for s in rows_of[0]]
    loads += [("C", 1, s) for s in rows_of[1][BPS:]] + [("C", i, s) for i in range(2, NS) for s in rows_of[i]]
    load_at = {key: q for q, key in enumerate(loads)}
    slot_of, turn_of, last_in_slot = [], [], []
    for phase, _, _ in loads:
        slot = (slot_of[-1] + 1) % (RING_C if phase == "C" else RING) if slot_of else 0
        earlier = [q for q, other in enumerate(slot_of) if other == slot]
        last_in_slot.append(earlier[-1] if earlier else None)
        turn_of.append(len(earlier) + 1)
        slot_of.append(slot)

    adds_at, blocks_at = {}, {}
    adds = blocks = 0
    for i in range(NS):
        for n, s in enumerate(pass_a_order(i)):
            adds += n > 0
            adds_at[load_at["A", i, s]] = adds + (n == 0)
            if s < BPS * i:
                blocks += 1
                blocks_at[load_at["A", i, s]] = blocks
        adds += BPS
    adds_per_strip = NB - 1
    assert adds == NS * adds_per_strip
    pieces_at = {}
    pieces = 0
    for q, (phase, i, _) in enumerate(loads):
        if phase == "B" and i < NS - 2:
            pieces += JT
            pieces_at[q] = pieces
        elif phase != "A":
            blocks += 1
            blocks_at[q] = blocks

    FIRST_SLOT, LAST_SLOT = GCN, DS * (NCH - 1) + RESIDUAL + 1
    slots = list(range(FIRST_SLOT - 1, LAST_SLOT))
    products = {g: [] for g in slots}
    mms = [[(i, s, a, c) for s in rows_of[i] for a in range(JT) for c in range(STRIP // MM)] for i in range(NS)]
    diagonal_1 = BPS * JT * STRIP // MM
    products[FIRST_SLOT - 1] = mms[1][:diagonal_1] + mms[0]
    mms[1] = mms[1][diagonal_1:]
    handover = {0: FIRST_SLOT}
    start, end = FIRST_SLOT, DS * CPS * (NS - 1) + GCN
    total, n = sum(len(m) for m in mms[1:]), 0
    for i in range(1, NS):
        for mm in mms[i]:
            products[max(start + n * (end - start) // total, handover[i - 1])].append(mm)
            n += 1
        handover[i] = min(start + n * (end - start) // total + 1, end)
        assert handover[i] <= DS * CPS * i + GCN
        assert i < 2 or handover[i] - 2 > DS * (CPS * (i - 1) - 1) + GCN
    block_end = {load_at["C", i, s]: g for g in slots for i, s, _, _ in products[g]}

    misc = []
    for g in range(FIRST_SLOT, LAST_SLOT):
        for stage, kinds in ((GCN, ["gcn"]), (OUT, ["out"]), (TRANSPOSE, ["tr"]), (XZ, ["xz0"]), (XZ + 1, ["xz1"]),
                             (XZ + 2, ["xz2"]), (XZ + 3, ["xz3"]), (DBC, ["dbc"]), (DT, ["dt0", "dt1"])):
            k = chunk_at(g, stage)
            if k is not None:
                misc += [(kind, k) for kind in kinds]
    misc_at = {key: m for m, key in enumerate(misc)}

    with ExitStack() as ctx:
        def sb(name, shape, dt=F32):
            return ctx.enter_context(nc.sbuf_tensor(name, shape, dt))

        def sem(name):
            return ctx.enter_context(nc.semaphore(name))

        ring = sb("ring", [P, RING, BLOCK])
        diag_h1 = sb("diag_h1", [P, BPS * BLOCK])
        diag = diag_h1[:, :].rearrange("p (b c) -> p b c", b=BPS)
        h1 = diag_h1[:, 0:N]
        arena_offset = nc.sbuf_base
        arena = sb("arena", [P, ARENA])
        h0 = arena[:, 0:N]
        adj_parts = nc.alloc_sbuf_tensor_at("adj_parts", [P, 2, 2, STRIP], F32R, offset=arena_offset + 4 * N)
        h_parts = nc.alloc_sbuf_tensor_at("h_parts", [P, 2, 2, 2, JT * F], F32R,
                                          offset=arena_offset + 4 * (N + 4 * STRIP))
        top = [N + 4 * STRIP + 8 * JT * F]

        def work(cols):
            top[0] += cols
            assert top[0] <= ARENA
            return arena[:, top[0] - cols:top[0]]

        l0_sums = [work(STRIP) for _ in range(2)]
        xs = [work(STRIP) for _ in range(2)]
        after_xs = top[0]
        rowacc = work(BLOCK)
        top[0] = after_xs
        s0 = work(STRIP)
        pre = work(STRIP)
        x1 = [work(STRIP) for _ in range(2)]
        l1_stage = work(STRIP)
        top[0] = 0

        def work2(*dims):
            size = 1
            for d in dims:
                size *= d
            v = work(size)
            if len(dims) == 2:
                v = v.rearrange("p (a b) -> p a b", a=dims[0])
            return v

        s1 = [work2(STRIP) for _ in range(2)]
        gbuf = work2(CT, F)
        h_t = work2(T)
        xcp = work2(HALVES, T + CONV)
        cv = work2(HALVES, T)
        u = [work2(HALVES, T) for _ in range(2)]
        sz = [work2(HALVES, T) for _ in range(2)]
        bcv = work2(T)
        dt = [work2(HALVES, T) for _ in range(2)]
        w = [work2(HALVES, T) for _ in range(2)]
        da = [work2(HALVES, T) for _ in range(2)]
        dbu = work2(HALVES, T)
        hs = [work2(HALVES, T) for _ in range(HSB - 2)]
        hs += [ring[:, RING - 1, b * HALVES * T:(b + 1) * HALVES * T].rearrange("p (a b) -> p a b", a=HALVES)
               for b in range(2)]
        csb = [work2(2, T) for _ in range(2)]
        yg = work2(HALVES, T)
        x1t = work2(CT, F)
        parts = [sb(f"parts{i}", [KD, T], F32R) for i in range(2)]

        ident = sb("ident", [P, P])
        pick = sb("pick", [KP, NBC], F32R)
        ones = sb("ones", [P, 1])
        w0t_sb = sb("w0t_sb", [P, F])
        b0_sb = sb("b0_sb", [P, F])
        gw_sb = sb("gw_sb", [P, F])
        gb_sb = sb("gb_sb", [P, F])
        ln_sb = sb("ln_sb", [P, 2])
        w_in_sb = sb("w_in_sb", [P, 2 * DI])
        conv_sb = sb("conv_sb", [P, HALVES, CONV])
        cols_sb = sb("cols_sb", [P, 3, HALVES])
        wx_sb = sb("wx_sb", [P, HALVES, KD])
        wdt_sb = sb("wdt_sb", [P, DI])
        wdt_parts = sb("wdt_parts", [KD, DI], F32R)
        a_sb = sb("a_sb", [P, HALVES, DS])
        wo_sb = sb("wo_sb", [P, HALVES, F])
        state = sb("state", [P, HALVES, DS])
        dcol = sb("dcol", [P, N // P])
        stats = sb("stats", [P, TPS, 6])
        mv = sb("mv", [P, TPS, 2])
        base = sb("base", [P, TPS])
        minus_half = sb("minus_half", [P, TPS])
        rstd = sb("rstd", [P, TPS])
        nmr = sb("nmr", [P, TPS])

        ps = ctx.enter_context(nc.psum_tensor("ps", [P, 8, MM], F32))
        acc0 = [ps[:, 0:2, :], ps[:, 2:4, :]]
        ps_deg = ps[:, 4, 0:TPS]
        acc1 = ps[:, 4:6, :]
        ps_w = ps[:, 6:8, :]
        acc_c = ps[:, 2:4, :]
        y_ps = ps[:, 0:2, :]
        b_ps = [ps[:, 4, :], ps[:, 5, :]]
        misc_ps = [ps[:, 6, :], ps[:, 7, :]]

        weights_in = sem("weights_in")
        ring_in = [sem(f"ring_in{i}") for i in range(RING)]
        diag_in = [sem(f"diag_in{i}") for i in range(BPS)]
        xs_in = [sem(f"xs_in{i}") for i in range(2)]
        cleared = sem("cleared")
        consts_done = sem("consts_done")
        wdt_low = sem("wdt_low")
        wdt_placed = sem("wdt_placed")
        wdt_ready = sem("wdt_ready")
        a_done = sem("a_done")
        dve_step = sem("dve_step")
        adds_done = sem("adds_done")
        blocks_done = sem("blocks_done")
        diag_done = sem("diag_done")
        fold_done = sem("fold_done")
        base_ready = sem("base_ready")
        pow_done = sem("pow_done")
        norm_ready = sem("norm_ready")
        normed = sem("normed")
        h0_ready = sem("h0_ready")
        part_ready = sem("part_ready")
        layer0_sum = sem("layer0_sum")
        s0_ready = sem("s0_ready")
        w_done = sem("w_done")
        x1_ready = sem("x1_ready")
        x1_out = [sem(f"x1_out{i}") for i in range(2)]
        l1_staged = sem("l1_staged")
        l1_out = sem("l1_out")
        l1_back = [sem(f"l1_back{i}") for i in range(2)]
        l0_out = [sem(f"l0_out{i}") for i in range(2)]
        l0_back = [sem(f"l0_back{i}") for i in range(2)]
        hi_ready = sem("hi_ready")
        lo_ready = sem("lo_ready")
        h_hi_ready = sem("h_hi_ready")
        h_lo_ready = sem("h_lo_ready")
        pieces_done = sem("pieces_done")
        s1_ready = sem("s1_ready")
        misc_full = sem("misc_full")
        misc_free = [sem(f"misc_free{i}") for i in range(2)]
        act_step = sem("act_step")
        relu_done = sem("relu_done")
        halo_done = sem("halo_done")
        tap0_done = sem("tap0_done")
        conv_done = sem("conv_done")
        u_ready = sem("u_ready")
        sz_ready = sem("sz_ready")
        bc_high = sem("bc_high")
        parts_ready = sem("parts_ready")
        ex_ready = sem("ex_ready")
        w1_ready = sem("w1_ready")
        log_ready = sem("log_ready")
        dt_ready = sem("dt_ready")
        b_ready = sem("b_ready")
        c_out = sem("c_out")
        c_in = [sem(f"c_in{i}") for i in range(2)]
        da_ready = sem("da_ready")
        dbu_done = sem("dbu_done")
        scan_done = sem("scan_done")
        state_saved = sem("state_saved")
        mult_done = sem("mult_done")
        pair_done = sem("pair_done")
        quad_done = sem("quad_done")
        nsum_done = sem("nsum_done")
        y_free = sem("y_free")
        yg_ready = sem("yg_ready")
        x1t_in = sem("x1t_in")
        out_done = sem("out_done")

        NORM_C = 2 * NS

        block = ctx.enter_context(nc.Block())

        def tile_of(h, t):
            return h[:, t * F:(t + 1) * F]

        def rows(v, n):
            return v.rearrange("p (t f) -> p t f", t=n)

        def halves(v):
            return v.rearrange("p (h c) -> p h c", c=MM)

        def misc_of(kind, k):
            return misc_ps[misc_at[kind, k] % 2]

        def evacuated(eng, kind, k):
            m = misc_at[kind, k]
            eng.wait_ge(misc_free[m % 2], m // 2 + 1)

        PAIRS_ADDED = (NCH - SPARED) * (DS // 2)

        def added_to_next(G):
            return G % (DS // 2) in QUADS and G < PAIRS_ADDED

        def quads_before(G):
            return sum(added_to_next(g) for g in range(G))

        def nsums_before(G):
            return G - quads_before(G)

        weight_loads = [
            (ident[:, :], ident_in), (w0t_sb[:, :], w0t), (b0_sb[:, :], b0.to_broadcast([P, F])),
            (gw_sb[:, :], gcn_w), (gb_sb[:, :], gcn_b.to_broadcast([P, F])),
            (ln_sb[:, 0:1], ln_g), (ln_sb[:, 1:2], ln_b), (w_in_sb[:, :], w_in),
            (conv_sb[:, :, :], conv_w), (cols_sb[:, 0, :], conv_b), (cols_sb[:, 1, :], b_dt),
            (cols_sb[:, 2, :], d_skip), (a_sb[:, :, :], a_log), (wo_sb[:, :, :], w_out),
        ]
        weight_loads += [(wx_sb[:, :, r:r + NBC], w_x[:, :, RANK:RANK + NBC]) for r in (0, LOW)]
        for r in (RANKS, RANKS + RANK, KP):
            weight_loads += [(wx_sb[:, :, r:r + RANK], w_x[:, :, 0:RANK]), (wdt_sb[r:r + RANK, :], w_dt)]
        n_weights = len(weight_loads)

        @block.sync
        def _(sp):
            def load(q):
                _, i, s = loads[q]
                old = last_in_slot[q]
                if old is not None:
                    if old in adds_at:
                        sp.wait_ge(adds_done, adds_at[old])
                    if old in blocks_at:
                        sp.wait_ge(blocks_done, blocks_at[old])
                    if old in pieces_at:
                        sp.wait_ge(lo_ready, pieces_at[old])
                    sp.wait_ge(ring_in[slot_of[q]], 16 * (turn_of[q] - 1))
                sp.dma_start(ring[:, slot_of[q], :], adj[s, i]).then_inc(ring_in[slot_of[q]], 16)

            for i in range(NS):
                for s in pass_a_order(i):
                    load(load_at["A", i, s])
                for b in range(BPS):
                    if i:
                        sp.wait_ge(adds_done, adds_per_strip * i)
                        sp.wait_ge(diag_done, i)
                        sp.wait_ge(diag_in[b], 16 * i)
                    sp.dma_start(diag[:, b, :], adj[BPS * i + b, i]).then_inc(diag_in[b], 16)
            first_c = load_at["C", 0, 0]
            for q in range(load_at["B", NS - 2, NB - 1], first_c):
                load(q)
            q = first_c
            for g in slots:
                pair = (g + 2) // 2
                if g % 2 == 0 and 0 <= pair < NCH * DS // 2:
                    k, n = divmod(2 * pair, DS)
                    sp.wait_ge(c_out, 16 * (k + 1))
                    if pair >= 2:
                        sp.wait_ge(mult_done, 2 * pair - 2)
                        sp.wait_ge(c_in[pair % 2], 16 * (pair // 2))
                    sp.dma_start(csb[pair % 2], c_dram[k:k + 1, n * T:(n + 2) * T].rearrange("a (n t) -> a n t", n=2)
                                 .to_broadcast([P, 2, T])).then_inc(c_in[pair % 2], 16)
                while q < len(loads) and block_end.get(last_in_slot[q], g) <= g:
                    load(q)
                    q += 1
            assert q == len(loads)

        @block.gpsimd
        def _(pool):
            nc.gpsimd.memset(wdt_sb[:, :], 0.0).then_inc(cleared, 1)
            nc.gpsimd.memset(wx_sb[:, :, RANKS:LOW], 0.0).then_inc(cleared, 1)
            nc.gpsimd.memset(ones[:, :], 1.0).then_inc(consts_done, 1)
            nc.gpsimd.memset(minus_half[:, :], -0.5).then_inc(consts_done, 1)
            nc.gpsimd.memset(state[:, :, :], 0.0).then_inc(consts_done, 1)

            def power(m, cols):
                pool.wait_ge(base_ready, m + 1)
                if m == 0:
                    pool.wait_ge(consts_done, 3)
                else:
                    pool.wait_ge(norm_ready, m)
                nc.gpsimd.tensor_tensor(rstd[:, 0:cols], base[:, 0:cols], minus_half[:, 0:cols],
                                        ALU.pow).then_inc(pow_done, 1)

            for m in range(3 * NS):
                power(m, TPS)

            for g in range(FIRST_SLOT, LAST_SLOT):
                normed_chunk = chunk_at(g, POWER)
                if normed_chunk is not None:
                    power(3 * NS + normed_chunk, CT)
                if 0 <= g < NCH * DS:
                    buf = hs[g % HSB]
                    pool.wait_ge(state_saved, g + 1)
                    pool.wait_ge(c_in[g // 2 % 2], 16 * (g // 4 + 1))
                    c_row = csb[g // 2 % 2][:, g % 2:g % 2 + 1, :].to_broadcast([P, HALVES, T])
                    nc.gpsimd.tensor_tensor(buf, buf, c_row, ALU.mult).then_inc(mult_done, 1)
                    if g % 2 and g // 2 < PAIRS_ADDED:
                        pool.wait_ge(mult_done, g + 1)
                        even = hs[(g - 1) % HSB]
                        nc.gpsimd.tensor_tensor(even, even, buf, ALU.add).then_inc(pair_done, 1)

        @block.vector
        def _(dve):
            steps = [0]

            def step(ins):
                steps[0] += 1
                ins.then_inc(dve_step, 1)
                dve.wait_ge(dve_step, steps[0])

            powers = [0]

            def tile_stats(tiles, first=0):
                for t, v in enumerate(tiles, first):
                    ins = nc.vector.bn_stats(stats[:, t, :], v)
                return ins

            def norm_stats(tiles, taken=0):
                n = len(tiles)
                step(tile_stats(tiles[taken:], taken))
                for t in range(n):
                    ins = nc.vector.bn_aggr(mv[:, t, :], stats[:, t, :])
                step(ins)
                powers[0] += 1
                nc.vector.tensor_scalar(base[:, 0:n], mv[:, 0:n, 1], LN_EPS, None, ALU.add).then_inc(base_ready, 1)

            def norm_bias(n):
                dve.wait_ge(pow_done, powers[0])
                nc.vector.scalar_tensor_tensor(nmr[:, 0:n], mv[:, 0:n, 0], -1.0, rstd[:, 0:n],
                                               ALU.mult, ALU.mult).then_inc(norm_ready, 1)

            def constants():
                dve.wait_ge(weights_in, 16 * n_weights)
                dve.wait_ge(consts_done, 3)
                for r, c in ((0, 0), (RANKS, 0), (LOW, LOW)):
                    nc.vector.tensor_copy(pick[r:r + NBC, :], ident[r:r + NBC, c:c + NBC])
                ranks = slice(RANKS, RANKS + RANK)
                step(nc.vector.tensor_copy(wdt_parts[ranks, :], wdt_sb[ranks, :]))
                nc.vector.tensor_tensor(l1_stage[ranks, 0:DI], wdt_sb[ranks, :], wdt_parts[ranks, :].bitcast(F32),
                                        ALU.subtract).then_inc(wdt_low, 1)
                dve.wait_ge(a_done, 1)
                step(nc.vector.tensor_scalar(a_sb[:, :, :], a_sb[:, :, :], -1.0, None, ALU.mult))

            total_adds = 0
            for i in range(NS):
                order = [("ring", load_at["A", i, s]) for s in pass_a_order(i)] + [("diag", b) for b in range(BPS)]

                def arrived(where):
                    kind, q = where
                    if kind == "ring":
                        dve.wait_ge(ring_in[slot_of[q]], 16 * turn_of[q])
                        return ring[:, slot_of[q], :]
                    dve.wait_ge(diag_in[q], 16 * (i + 1))
                    return diag[:, q, :]

                if i:
                    dve.wait_ge(fold_done, i)
                first, second = arrived(order[0]), arrived(order[1])
                total_adds += 1
                nc.vector.tensor_tensor(rowacc, first, second, ALU.add).then_inc(adds_done, 1)
                for n, where in enumerate(order[2:]):
                    if n == 4:
                        if i == 0:
                            constants()
                        if i == 1:
                            dve.wait_ge(wdt_placed, 16)
                            nc.vector.tensor_copy(wdt_parts[:, :], wdt_sb[0:KD, :]).then_inc(wdt_ready, 1)
                        dve.wait_ge(xs_in[i % 2], 16 * (i // 2 + 1))
                        if i:
                            dve.wait_ge(normed, i)
                        norm_stats([tile_of(xs[i % 2], t) for t in range(TPS)])
                    if n == 6:
                        norm_bias(TPS)
                    v = arrived(where)
                    dve.wait_ge(adds_done, total_adds)
                    total_adds += 1
                    nc.vector.tensor_tensor(rowacc, rowacc, v, ALU.add).then_inc(adds_done, 1)
                dve.wait_ge(fold_done, i + 1)
                dve.wait_ge(normed, i + 1)
                powers[0] += 1
                nc.vector.tensor_scalar(base[:, :], ps_deg, DEG_EPS, None, ALU.add).then_inc(base_ready, 1)
                dve.wait_ge(pow_done, powers[0])
                deg = dcol[:, i * TPS:(i + 1) * TPS]
                nc.vector.tensor_copy(deg, rstd[:, :]).then_inc(norm_ready, 1)
                dve.wait_ge(norm_ready, powers[0])
                hv = rows(h0[:, i * STRIP:(i + 1) * STRIP], TPS)
                nc.vector.tensor_tensor(hv, hv, deg.unsqueeze(2).to_broadcast([P, TPS, F]),
                                        ALU.mult).then_inc(h0_ready, 1)

            def low_part(r, q, a):
                buf, blk = r % 2, r // JT
                if a == 0:
                    s = loads[q][2]
                    dve.wait_ge(h_hi_ready, 2 * (blk + 1))
                    for layer, h in enumerate((h0, h1)):
                        nc.vector.tensor_tensor(h_parts[:, blk % 2, layer, 1, :],
                                                h[:, JT * s * F:JT * (s + 1) * F],
                                                h_parts[:, blk % 2, layer, 0, :].bitcast(F32), ALU.subtract)\
                            .then_inc(h_lo_ready, 1)
                dve.wait_ge(hi_ready, r + 1)
                nc.vector.tensor_tensor(adj_parts[:, buf, 1, :], ring[:, slot_of[q], a * STRIP:(a + 1) * STRIP],
                                        adj_parts[:, buf, 0, :].bitcast(F32), ALU.subtract).then_inc(lo_ready, 1)

            def complete(n, stage):
                i = NS - 1 - n
                if stage == 0 and n:
                    dve.wait_ge(layer0_sum, n)
                    dve.wait_ge(l0_back[i % 2], 16 * ((n + 1) // 2))
                    dve.wait_ge(w_done, n)
                    nc.vector.tensor_tensor(halves(s0), acc0[i % 2], halves(l0_sums[i % 2]), ALU.add)\
                        .then_inc(s0_ready, 1)
                if stage == 1:
                    dve.wait_ge(w_done, n + 1)
                    deg = dcol[:, i * TPS:(i + 1) * TPS].unsqueeze(2).to_broadcast([P, TPS, F])
                    pv = rows(pre, TPS)
                    step(nc.vector.tensor_tensor(pv, ps_w.rearrange("p b (t f) -> p (b t) f", f=F), deg, ALU.mult))
                if stage == 2:
                    pv = rows(pre, TPS)
                    step(nc.vector.tensor_tensor(pv, pv, b0_sb[:, :].unsqueeze(1).to_broadcast([P, TPS, F]),
                                                 ALU.add))
                if stage == 3:
                    dve.wait_ge(xs_in[n % 2], 16 * (NS // 2 + n // 2 + 1))
                    if n >= 2:
                        dve.wait_ge(x1_out[n % 2], 16 * (n // 2))
                    if n:
                        dve.wait_ge(normed, NS + n)
                    nc.vector.scalar_tensor_tensor(x1[n % 2], pre, 0.0, xs[n % 2], ALU.max, ALU.add)\
                        .then_inc(x1_ready, 1)
                    dve.wait_ge(x1_ready, n + 1)
                tiles = [tile_of(x1[n % 2], t) for t in range(TPS)]
                if stage == 4:
                    tile_stats(tiles[:TPS // 2])
                if stage == 5:
                    norm_stats(tiles, TPS // 2)
                if stage == 6:
                    norm_bias(TPS)

            for stage in range(7):
                complete(0, stage)
            r = 0
            for n, i in enumerate(reversed(range(NS - 2)), 1):
                strip_pieces = [(load_at["B", i, s], a) for s in reversed(range(BPS * (i + 1), NB)) for a in range(JT)]
                for m, (q, a) in enumerate(strip_pieces):
                    if r >= 2:
                        dve.wait_ge(pieces_done, r - 1)
                    low_part(r, q, a)
                    r += 1
                    complete(n, m)
            for stage in range(7):
                complete(NS - 1, stage)

            for g in range(FIRST_SLOT, LAST_SLOT):
                for i in range(NS):
                    if handover[i] != g:
                        continue
                    dve.wait_ge(blocks_done, blocks_at[load_at["C", i, rows_of[i][-1]]])
                    if i < NS - 1:
                        dve.wait_ge(l1_back[i % 2], 16 * (i // 2 + 1))
                        nc.vector.tensor_tensor(halves(s1[i % 2]), acc_c if i else y_ps, halves(s1[i % 2]), ALU.add)\
                            .then_inc(s1_ready, 1)
                    else:
                        dve.wait_ge(misc_full, misc_at["gcn", CPS * (i - 1) - 1] + 1)
                        nc.vector.tensor_copy(halves(s1[i % 2]), acc_c).then_inc(s1_ready, 1)
                if 0 <= g < NCH * DS:
                    k, n = divmod(g, DS)
                    if n == 0:
                        dve.wait_ge(dt_ready, 2 * (k + 1))
                    dve.wait_ge(b_ready, g + 1)
                    for h in range(HALVES):
                        if g:
                            dve.wait_ge(scan_done, 2 * g - 1 + h)
                        nc.vector.tensor_tensor(dbu[:, h, :], w[k % 2][:, h, :], b_ps[g % 2], ALU.mult)\
                            .then_inc(dbu_done, 1)
                    dve.wait_ge(da_ready, g + 1)
                    if k:
                        dve.wait_ge(state_saved, g - DS + 1)
                    if g >= HSB:
                        G = (g - HSB) // 2
                        if added_to_next(G):
                            dve.wait_ge(quad_done, quads_before(G + 1))
                        else:
                            dve.wait_ge(nsum_done, nsums_before(G + 1))
                    for h in range(HALVES):
                        dve.wait_ge(dbu_done, 2 * g + 1 + h)
                        nc.vector.tensor_tensor_scan(hs[g % HSB][:, h, :], da[g % 2][:, h, :], dbu[:, h, :],
                                                     state[:, h, n:n + 1], ALU.mult, ALU.add).then_inc(scan_done, 1)

                G, odd = divmod(g - QUAD, 2)
                if not odd and 0 <= G < NCH * DS // 2 and added_to_next(G):
                    dve.wait_ge(pair_done, G + 2)
                    both = hs[(2 * G + 2) % HSB]
                    nc.vector.tensor_tensor(both, both, hs[2 * G % HSB], ALU.add).then_inc(quad_done, 1)

                k = chunk_at(g, BIAS)
                if k is not None:
                    dve.wait_ge(misc_full, misc_at["gcn", k] + 1)
                    if k:
                        dve.wait_ge(misc_full, misc_at["tr", k - 1] + 1)
                    nc.vector.tensor_tensor(gbuf, rows(misc_of("gcn", k), CT),
                                            gb_sb[:, :].unsqueeze(1).to_broadcast([P, CT, F]), ALU.add)\
                        .then_inc(misc_free[misc_at["gcn", k] % 2], 1)
                k = chunk_at(g, STATS)
                if k is not None:
                    dve.wait_ge(normed, NORM_C + k)
                    dve.wait_ge(relu_done, k + 1)
                    norm_stats([gbuf[:, t, :] for t in range(CT)])
                k = chunk_at(g, NORMALISE)
                if k is not None:
                    norm_bias(CT)
                k = chunk_at(g, HALO)
                if k is not None:
                    if k:
                        ins = nc.vector.tensor_copy(xcp[:, :, 1:CONV], xcp[:, :, T + 1:T + CONV])
                    else:
                        ins = nc.vector.memset(xcp[:, :, 1:CONV], 0.0)
                    ins.then_inc(halo_done, 1)
                for part, stage in enumerate(CONVOLVE):
                    k = chunk_at(g, stage)
                    if k is None:
                        continue
                    tap = part + 1
                    for h in range(HALVES):
                        if part:
                            dve.wait_ge(conv_done, HALVES * ((CONV - 1) * k + tap - 2) + h + 1)
                        else:
                            dve.wait_ge(tap0_done, HALVES * k + h + 1)
                        nc.vector.scalar_tensor_tensor(cv[:, h, :], xcp[:, h, 1 + tap:1 + tap + T],
                                                       conv_sb[:, h, tap:tap + 1], cv[:, h, :], ALU.mult, ALU.add)\
                            .then_inc(conv_done, 1)
                k = chunk_at(g, SPLIT)
                if k is not None:
                    dve.wait_ge(bc_high, k + 1)
                    low = parts[k % 2][LOW:KD, :]
                    nc.vector.tensor_tensor(low, bcv[LOW:KD, :], low.bitcast(F32), ALU.subtract)\
                        .then_inc(parts_ready, 1)
                k = chunk_at(g, SOFTPLUS)
                if k is not None:
                    ex, w1 = w[k % 2], dt[k % 2]
                    dve.wait_ge(ex_ready, k + 1)
                    nc.vector.scalar_tensor_tensor(ex, w1, -1.0, ex, ALU.add, ALU.subtract).then_inc(w1_ready, 1)
                k = chunk_at(g, TIME_STEP)
                if k is not None:
                    ex, w1 = w[k % 2], dt[k % 2]
                    dve.wait_ge(w1_ready, k + 1)
                    step(nc.vector.scalar_tensor_tensor(ex, cv, 0.0, ex, ALU.max, ALU.subtract))
                    dve.wait_ge(log_ready, k + 1)
                    nc.vector.tensor_tensor(w1, ex, w1, ALU.add).then_inc(dt_ready, 1)
                k = chunk_at(g, WEIGHTED_U)
                if k is not None:
                    dve.wait_ge(dt_ready, 2 * k + 1)
                    dve.wait_ge(u_ready, k + 1)
                    nc.vector.tensor_tensor(w[k % 2], dt[k % 2], u[k % 2], ALU.mult).then_inc(dt_ready, 1)
                k = chunk_at(g, SKIP)
                if k is not None:
                    dve.wait_ge(nsum_done, nsums_before(DS // 2 * (k + 1)))
                    if k:
                        dve.wait_ge(misc_full, misc_at["out", k - 1] + 1)
                    for h in range(HALVES):
                        ins = nc.vector.scalar_tensor_tensor(yg[:, h, :], u[k % 2][:, h, :], cols_sb[:, 2, h:h + 1],
                                                             y_ps[:, h, :], ALU.mult, ALU.add)
                    ins.then_inc(y_free, 1)
                k = chunk_at(g, GATE)
                if k is not None:
                    dve.wait_ge(y_free, k + 1)
                    dve.wait_ge(sz_ready, k + 1)
                    nc.vector.tensor_tensor(yg, yg, sz[k % 2], ALU.mult).then_inc(yg_ready, 1)
                k = chunk_at(g, RESIDUAL)
                if k is not None:
                    dve.wait_ge(misc_full, misc_at["out", k] + 1)
                    dve.wait_ge(x1t_in, 16 * (k + 1))
                    nc.vector.tensor_tensor(x1t, rows(misc_of("out", k), CT), x1t, ALU.add)\
                        .then_inc(misc_free[misc_at["out", k] % 2], 1)

        @block.tensor
        def _(pe):
            def arrived(q):
                pe.wait_ge(ring_in[slot_of[q]], 16 * turn_of[q])
                return ring[:, slot_of[q], :]

            def product(acc, h, s, blk, start, stop):
                for a in range(JT):
                    for c in range(STRIP // MM):
                        last = nc.tensor.matmul(acc[:, c, :], tile_of(h, JT * s + a),
                                                blk[:, a * STRIP + c * MM:a * STRIP + (c + 1) * MM],
                                                start=start and a == 0, stop=stop and a == JT - 1)
                return last

            pe.wait_ge(consts_done, 3)
            def diagonal(i):
                pe.wait_ge(h0_ready, i + 1)
                for b in range(BPS):
                    pe.wait_ge(diag_in[b], 16 * (i + 1))
                    last = product(acc0[i % 2], h0, BPS * i + b, diag[:, b, :], i == 0 and b == 0, b == BPS - 1)
                last.then_inc(diag_done, 1)

            def fold(i):
                pe.wait_ge(adds_done, adds_per_strip * (i + 1))
                if i:
                    pe.wait_ge(h0_ready, i)
                for t in range(TPS):
                    for a in range(JT):
                        last = nc.tensor.matmul(ps_deg[:, t:t + 1],
                                                rowacc[:, a * STRIP + t * P:a * STRIP + (t + 1) * P], ones[:, :],
                                                start=a == 0, stop=a == JT - 1)
                last.then_inc(fold_done, 1)

            for i in range(NS):
                lower = [s for s in pass_a_order(i) if s < BPS * i]
                if i >= 2:
                    pe.wait_ge(part_ready, i - 1)
                kept = KEPT if i == NS - 1 else 0
                for n, s in enumerate(lower):
                    if n == min(AHEAD, len(lower) - BPS):
                        diagonal(i - 1)
                    if n == len(lower) - kept:
                        fold(i)
                    pe.wait_ge(h0_ready, s // BPS + 1)
                    product(acc0[i % 2], h0, s, arrived(load_at["A", i, s]), n == 0, False)\
                        .then_inc(blocks_done, 1)
                if not kept:
                    fold(i)
            diagonal(NS - 1)

            def through_w(n, i):
                if n == 0:
                    pe.wait_ge(part_ready, NS)
                    src = l0_sums[i % 2]
                else:
                    pe.wait_ge(s0_ready, n)
                    pe.wait_ge(x1_ready, n)
                    src = s0
                for t in range(TPS):
                    last = nc.tensor.matmul(ps_w[:, t // CT, t % CT * F:(t % CT + 1) * F],
                                            src[:, t * P:(t + 1) * P], w0t_sb[:, :], start=True, stop=True)
                last.then_inc(w_done, 1)

            pe.wait_ge(weights_in, 16 * n_weights)
            through_w(0, NS - 1)
            firsts = list(reversed(range(BPS * (NS - 1), NB)))
            for layer, acc, h in ((0, acc0[NS % 2], h0), (1, acc1, h1)):
                if layer:
                    pe.wait_ge(normed, NS + 1)
                for s in firsts:
                    last = product(acc, h, s, arrived(load_at["B", NS - 2, s]), s == firsts[0], s == firsts[-1])
                    if layer:
                        last.then_inc(blocks_done, 1)
                if layer == 0:
                    last.then_inc(layer0_sum, 1)

            def split_product(acc, r, a, layer, start, stop):
                buf, blk = r % 2, r // JT
                for adj_part, h_part in ((0, 0), (0, 1), (1, 0)):
                    if adj_part:
                        pe.wait_ge(lo_ready, r + 1)
                    for c in range(STRIP // MM):
                        last = nc.tensor.matmul(
                            acc[:, c, :], h_parts[:, blk % 2, layer, h_part, a * F:(a + 1) * F],
                            adj_parts[:, buf, adj_part, c * MM:(c + 1) * MM],
                            start=start and (adj_part, h_part) == (0, 0), stop=stop and adj_part == 1)
                return last

            r = 0
            for n, i in enumerate(reversed(range(NS - 2)), 1):
                strip_pieces = [(s, a) for s in reversed(range(BPS * (i + 1), NB)) for a in range(JT)]
                if n >= 2:
                    pe.wait_ge(s0_ready, n - 1)
                for m, (s, a) in enumerate(strip_pieces):
                    start, stop = m == 0, m == len(strip_pieces) - 1
                    pe.wait_ge(hi_ready, r + 1)
                    pe.wait_ge(h_lo_ready, 2 * (r // JT + 1))
                    last = split_product(acc0[i % 2], r, a, 0, start, stop)
                    if stop:
                        last.then_inc(layer0_sum, 1)
                    if start:
                        pe.wait_ge(l1_staged, n)
                    split_product(acc1, r, a, 1, start, stop).then_inc(pieces_done, 1)
                    r += 1
                    if m == 0:
                        through_w(n, i + 1)
            through_w(NS - 1, 0)

            def c_products(mms):
                for i, s, a, c in mms:
                    q = load_at["C", i, s]
                    blk = arrived(q) if (a, c) == (0, 0) else ring[:, slot_of[q], :]
                    first, last_s = s == rows_of[i][0], s == rows_of[i][-1]
                    if first and (a, c) == (0, 0):
                        if i < 2:
                            pe.wait_ge(normed, NORM_C - i)
                        else:
                            pe.wait_ge(s1_ready, i)
                    last = nc.tensor.matmul((acc_c if i else y_ps)[:, c, :], tile_of(h1, JT * s + a),
                                            blk[:, a * STRIP + c * MM:a * STRIP + (c + 1) * MM],
                                            start=first and a == 0, stop=last_s and a == JT - 1)
                    if (a, c) == (JT - 1, STRIP // MM - 1):
                        last.then_inc(blocks_done, 1)

            def use_misc(key):
                m = misc_at[key]
                if m >= 2:
                    pe.wait_ge(misc_free[m % 2], m // 2)
                return misc_ps[m % 2]

            c_products(products[FIRST_SLOT - 1])
            for g in range(FIRST_SLOT, LAST_SLOT):
                if 0 <= g + 1 < NCH * DS:
                    kk, nn = divmod(g + 1, DS)
                    pe.wait_ge(parts_ready, kk + 1)
                    if g + 1 >= 2:
                        pe.wait_ge(dbu_done, HALVES * g)
                    pv = parts[kk % 2]
                    nc.tensor.matmul(b_ps[(g + 1) % 2], pick[:, nn:nn + 1].to_broadcast([KP, P]), pv[0:KP, :],
                                     start=True, stop=True).then_inc(b_ready, 1)
                G, odd = divmod(g - NSUM, 2)
                if not odd and 0 <= G < NCH * DS // 2:
                    pair = G % (DS // 2)
                    if not added_to_next(G):
                        terms = [hs[2 * G % HSB]]
                        if G >= PAIRS_ADDED:
                            pe.wait_ge(mult_done, 2 * G + 2)
                            terms.append(hs[(2 * G + 1) % HSB])
                        elif pair and added_to_next(G - 1):
                            pe.wait_ge(quad_done, quads_before(G))
                        else:
                            pe.wait_ge(pair_done, G + 1)
                        first = all(added_to_next(g) for g in range(G - pair, G))
                        if first and G >= DS // 2:
                            pe.wait_ge(y_free, G // (DS // 2))
                        for j, term in enumerate(terms):
                            for h in range(HALVES):
                                last = nc.tensor.matmul(y_ps[:, h, :], ident[:, :], term[:, h, :],
                                                        start=first and j == 0,
                                                        stop=pair == DS // 2 - 1 and j == len(terms) - 1)
                        last.then_inc(nsum_done, 1)
                k = chunk_at(g, GCN)
                if k is not None:
                    pe.wait_ge(s1_ready, k // CPS + 1)
                    m_ps = use_misc(("gcn", k))
                    for t in range(CT):
                        c = k % CPS * T + t * P
                        last = nc.tensor.matmul(m_ps[:, t * F:(t + 1) * F], s1[k // CPS % 2][:, c:c + P],
                                                gw_sb[:, :], start=True, stop=True)
                    last.then_inc(misc_full, 1)
                k = chunk_at(g, OUT)
                if k is not None:
                    pe.wait_ge(yg_ready, k + 1)
                    m_ps = use_misc(("out", k))
                    for t in range(CT):
                        for h in range(HALVES):
                            last = nc.tensor.matmul(m_ps[:, t * F:(t + 1) * F], yg[:, h, t * P:(t + 1) * P],
                                                    wo_sb[:, h, :], start=h == 0, stop=h == HALVES - 1)
                    last.then_inc(misc_full, 1)
                k = chunk_at(g, TRANSPOSE)
                if k is not None:
                    pe.wait_ge(normed, NORM_C + k + 1)
                    m_ps = use_misc(("tr", k))
                    for t in range(CT):
                        last = nc.tensor.transpose(m_ps[:, t * P:(t + 1) * P], gbuf[:, t, :], ident[:, :])
                    last.then_inc(misc_full, 1)
                for c in range(2 * HALVES):
                    k = chunk_at(g, XZ + c)
                    if k is not None:
                        evacuated(pe, "tr", k)
                        m_ps = use_misc((f"xz{c}", k))
                        nc.tensor.matmul(m_ps, w_in_sb[:, c * P:(c + 1) * P], h_t, start=True, stop=True)\
                            .then_inc(misc_full, 1)
                k = chunk_at(g, DBC)
                if k is not None:
                    pe.wait_ge(u_ready, k + 1)
                    m_ps = use_misc(("dbc", k))
                    for h in range(HALVES):
                        last = nc.tensor.matmul(m_ps[0:KD, :], wx_sb[:, h, :], u[k % 2][:, h, :],
                                                start=h == 0, stop=h == HALVES - 1)
                    last.then_inc(misc_full, 1)
                k = chunk_at(g, DT)
                if k is not None:
                    for h in range(HALVES):
                        pe.wait_ge(wdt_ready, 1)
                        pe.wait_ge(parts_ready, k + 1)
                        m_ps = use_misc((f"dt{h}", k))
                        nc.tensor.matmul(m_ps, wdt_parts[:, h * P:(h + 1) * P], parts[k % 2][:, :],
                                         start=True, stop=True).then_inc(misc_full, 1)
                c_products(products[g])

        @block.scalar
        def _(act):
            act.wait_ge(cleared, 2)
            for dst, src in weight_loads:
                act.dma_start(dst, src).then_inc(weights_in, 16)

            def load_xs(n, i):
                act.dma_start(xs[n % 2], x[:, i * STRIP:(i + 1) * STRIP]).then_inc(xs_in[n % 2], 16)

            def normalise(src, dst, n, func):
                for t in range(n):
                    last = nc.scalar.activation(dst[t], src[t], func, bias=nmr[:, t:t + 1], scale=rstd[:, t:t + 1])
                last.then_inc(normed, 1)

            load_xs(0, 0)
            load_xs(1, 1)
            act.wait_ge(weights_in, 16 * n_weights)
            nc.scalar.activation(a_sb[:, :, :], a_sb[:, :, :], ACT.Exp).then_inc(a_done, 1)

            def move_part(i):
                act.wait_ge(diag_done, i + 1)
                if i >= 2:
                    act.wait_ge(l0_out[i % 2], 16 * (i // 2))
                nc.scalar.activation(halves(l0_sums[i % 2]), acc0[i % 2], ACT.Copy).then_inc(part_ready, 1)
                if i < NS - 1:
                    act.wait_ge(part_ready, i + 1)
                    act.dma_start(lower0_dram[:, i * STRIP:(i + 1) * STRIP], l0_sums[i % 2])\
                        .then_inc(l0_out[i % 2], 16)

            for i in range(NS):
                act.wait_ge(norm_ready, 2 * i + 1)
                normalise([tile_of(xs[i % 2], t) for t in range(TPS)],
                          [tile_of(h0, i * TPS + t) for t in range(TPS)], TPS, ACT.Relu)
                act.wait_ge(normed, i + 1)
                m = i + 2
                load_xs(m, m if m < NS else 2 * NS - 1 - m)
                if i == 0:
                    act.wait_ge(wdt_low, 1)
                    act.dma_start(wdt_sb[RANKS + RANK:RANKS + 2 * RANK, :], l1_stage[RANKS:RANKS + RANK, 0:DI])\
                        .then_inc(wdt_placed, 16)
                if i:
                    move_part(i - 1)
            move_part(NS - 1)

            def load_l0(n):
                i = NS - 1 - n
                act.dma_start(l0_sums[i % 2], lower0_dram[:, i * STRIP:(i + 1) * STRIP]).then_inc(l0_back[i % 2], 16)

            for b in range(2):
                act.wait_ge(l0_out[b], 16 * (NS // 2 - b))
            load_l0(1)

            def high_part(r, q, a):
                buf, blk = r % 2, r // JT
                if r >= 2:
                    act.wait_ge(pieces_done, r - 1)
                if a == 0:
                    s = loads[q][2]
                    for layer, h in enumerate((h0, h1)):
                        if layer:
                            act.wait_ge(normed, NS + NS - s // BPS)
                        nc.scalar.activation(h_parts[:, blk % 2, layer, 0, :], h[:, JT * s * F:JT * (s + 1) * F],
                                             ACT.Copy).then_inc(h_hi_ready, 1)
                    act.wait_ge(ring_in[slot_of[q]], 16 * turn_of[q])
                nc.scalar.activation(adj_parts[:, buf, 0, :], ring[:, slot_of[q], a * STRIP:(a + 1) * STRIP],
                                     ACT.Copy).then_inc(hi_ready, 1)

            def layer1_input(n):
                i = NS - 1 - n
                act.wait_ge(norm_ready, 2 * NS + n + 1)
                if n == 0:
                    act.wait_ge(diag_done, NS)
                normalise([tile_of(x1[n % 2], t) for t in range(TPS)],
                          [tile_of(h1, i * TPS + t) for t in range(TPS)], TPS, ACT.Relu)
                act.dma_start(x1_dram[:, i * STRIP:(i + 1) * STRIP], x1[n % 2]).then_inc(x1_out[n % 2], 16)
                m = n + 2
                if m < NS:
                    load_xs(m, NS - 1 - m)
                    if n:
                        act.wait_ge(s0_ready, n)
                    else:
                        act.wait_ge(w_done, 1)
                    load_l0(m)

            def move_layer1(n, i):
                q = load_at["B", i, BPS * (i + 1)]
                if n:
                    act.wait_ge(pieces_done, pieces_at[q])
                else:
                    act.wait_ge(blocks_done, blocks_at[q])
                if n:
                    act.wait_ge(l1_out, 16 * n)
                nc.scalar.activation(halves(l1_stage), acc1, ACT.Copy).then_inc(l1_staged, 1)
                act.wait_ge(l1_staged, n + 1)
                act.dma_start(upper1_dram[:, i * STRIP:(i + 1) * STRIP], l1_stage).then_inc(l1_out, 16)

            layer1_input(0)
            r = 0
            for n, i in enumerate(reversed(range(NS - 2)), 1):
                strip_pieces = [(load_at["B", i, s], a) for s in reversed(range(BPS * (i + 1), NB)) for a in range(JT)]
                for m, (q, a) in enumerate(strip_pieces):
                    high_part(r, q, a)
                    r += 1
                    if m == (1 if n == 1 else 0):
                        move_layer1(n - 1, i + 1)
                    if m == 7:
                        layer1_input(n)
            move_layer1(NS - 2, 0)
            layer1_input(NS - 1)

            for b in range(2):
                act.wait_ge(x1_out[b], 16 * NS // 2)
            act.wait_ge(l1_out, 16 * (NS - 1))
            act.wait_ge(w_done, NS)
            act.wait_ge(normed, NORM_C)

            def evacuate(key, dst, **more):
                act.wait_ge(misc_full, misc_at[key] + 1)
                src = misc_of(*key)[0:dst.shape[0], :]
                nc.scalar.activation(dst, src, ACT.Identity if more else ACT.Copy, **more)\
                    .then_inc(misc_free[misc_at[key] % 2], 1)

            for g in range(FIRST_SLOT, LAST_SLOT):
                if 1 <= g <= NCH * DS:
                    act.wait_ge(scan_done, 2 * g)
                    n = (g - 1) % DS
                    nc.scalar.activation(state[:, :, n:n + 1], hs[(g - 1) % HSB][:, :, T - 1:T], ACT.Copy)\
                        .then_inc(state_saved, 1)
                if 0 <= g + 1 < NCH * DS:
                    k, n = divmod(g + 1, DS)
                    if n == 0:
                        act.wait_ge(dt_ready, 2 * k + 1)
                    for h in range(HALVES):
                        last = nc.scalar.activation(da[(g + 1) % 2][:, h, :], dt[k % 2][:, h, :], ACT.Exp,
                                                    scale=a_sb[:, h, n:n + 1])
                    last.then_inc(da_ready, 1)
                for i in range(NS - 1):
                    if max(handover[i] - 2, FIRST_SLOT) == g:
                        if i >= 2:
                            act.wait_ge(misc_full, misc_at["gcn", CPS * (i - 1) - 1] + 1)
                        act.dma_start(s1[i % 2], upper1_dram[:, i * STRIP:(i + 1) * STRIP])\
                            .then_inc(l1_back[i % 2], 16)
                k = chunk_at(g, LOAD_X1)
                if k is not None:
                    act.wait_ge(out_done, 16 * k)
                    act.dma_start(x1t, rows(x1_dram[:, k * T:(k + 1) * T], CT)).then_inc(x1t_in, 16)
                k = chunk_at(g, BIAS)
                if k is not None:
                    evacuated(act, "gcn", k)
                    nc.scalar.activation(gbuf, gbuf, ACT.Relu).then_inc(relu_done, 1)
                k = chunk_at(g, NORMALISE)
                if k is not None:
                    act.wait_ge(norm_ready, 3 * NS + k + 1)
                    g4 = [gbuf[:, t, :] for t in range(CT)]
                    normalise(g4, g4, CT, ACT.Identity)
                k = chunk_at(g, TRANSPOSE)
                if k is not None:
                    evacuate(("tr", k), h_t, scale=ln_sb[:, 0:1], bias=ln_sb[:, 1:2])
                for c in range(2 * HALVES):
                    k = chunk_at(g, XZ + c)
                    if k is None:
                        continue
                    if c < HALVES:
                        act.wait_ge(conv_done, HALVES * (CONV - 1) * k)
                        act.wait_ge(halo_done, k + 1)
                        evacuate((f"xz{c}", k), xcp[:, c, CONV:CONV + T])
                        evacuated(act, f"xz{c}", k)
                        act.wait_ge(dt_ready, 2 * k)
                        nc.scalar.activation(cv[:, c, :], xcp[:, c, 1:1 + T], ACT.Identity,
                                             scale=conv_sb[:, c, 0:1], bias=cols_sb[:, 0, c:c + 1])\
                            .then_inc(tap0_done, 1)
                    else:
                        if k >= 2:
                            act.wait_ge(yg_ready, k - 1)
                        evacuate((f"xz{c}", k), sz[k % 2][:, c - HALVES, :])
                k = chunk_at(g, SILU)
                if k is not None:
                    act.wait_ge(conv_done, HALVES * (CONV - 1) * (k + 1))
                    nc.scalar.activation(u[k % 2], cv, ACT.Silu).then_inc(u_ready, 1)
                    evacuated(act, "xz3", k)
                    nc.scalar.activation(sz[k % 2], sz[k % 2], ACT.Silu).then_inc(sz_ready, 1)
                k = chunk_at(g, DBC)
                if k is not None:
                    if k:
                        act.wait_ge(parts_ready, k)
                        act.wait_ge(c_out, 16 * k)
                    evacuate(("dbc", k), bcv[0:KD, :])
                    evacuated(act, "dbc", k)
                    nc.scalar.activation(parts[k % 2][:, :], bcv[0:KD, :], ACT.Copy).then_inc(bc_high, 1)
                    act.dma_start(c_dram[k:k + 1, :].rearrange("a (n t) -> (a n) t", n=DS), bcv[DS:2 * DS, :])\
                        .then_inc(c_out, 16)
                k = chunk_at(g, DT)
                if k is not None:
                    ex, w1 = w[k % 2], dt[k % 2]
                    for h in range(HALVES):
                        evacuate((f"dt{h}", k), cv[:, h, :], bias=cols_sb[:, 1, h:h + 1], scale=1.0)
                    evacuated(act, "dt1", k)
                    nc.scalar.activation(ex, cv, ACT.Abs).then_inc(act_step, 1)
                    act.wait_ge(act_step, 2 * k + 1)
                    nc.scalar.activation(ex, ex, ACT.Exp, scale=-1.0).then_inc(act_step, 1)
                    act.wait_ge(act_step, 2 * k + 2)
                    nc.scalar.activation(w1, ex, ACT.Identity, bias=ones[:, 0:1]).then_inc(ex_ready, 1)
                k = chunk_at(g, SOFTPLUS)
                if k is not None:
                    act.wait_ge(w1_ready, k + 1)
                    w1 = dt[k % 2]
                    nc.scalar.activation(w1, w1, ACT.Ln).then_inc(log_ready, 1)
                k = chunk_at(g, RESIDUAL)
                if k is not None:
                    evacuated(act, "out", k)
                    act.dma_start(rows(out[:, k * T:(k + 1) * T], CT), x1t).then_inc(out_done, 16)
            act.wait_ge(out_done, 16 * NCH)


def kernel(x, adj, L0_gnn_W, L0_gnn_b, L1_gnn_gcn_w, L1_gnn_gcn_b, L1_gnn_ln_g, L1_gnn_ln_b, L1_gnn_w_in,
           L1_gnn_conv_w, L1_gnn_conv_b, L1_gnn_w_xp, L1_gnn_w_dt, L1_gnn_b_dt, L1_gnn_A_log, L1_gnn_D_skip,
           L1_gnn_w_out):
    import numpy as np
    import concourse.bacc as bacc
    from concourse.bass_utils import run_bass_kernel_spmd

    def by_halves(a):
        a = np.asarray(a)
        return a.reshape(HALVES, P, -1).transpose(1, 0, 2)

    def column(a):
        return np.asarray(a).reshape(P, 1)

    laid_out = {
        "adj": np.asarray(adj).reshape(NS, STRIP, NB, JT, P).transpose(2, 0, 4, 3, 1).reshape(NB, NS, P, BLOCK),
        "x": np.asarray(x).reshape(N // P, P, F).transpose(1, 0, 2).reshape(P, N),
        "w0t": np.asarray(L0_gnn_W).T,
        "b0": np.asarray(L0_gnn_b).reshape(1, F),
        "gcn_w": L1_gnn_gcn_w,
        "gcn_b": np.asarray(L1_gnn_gcn_b).reshape(1, F),
        "ln_g": column(L1_gnn_ln_g),
        "ln_b": column(L1_gnn_ln_b),
        "w_in": L1_gnn_w_in,
        "conv_w": by_halves(L1_gnn_conv_w),
        "conv_b": by_halves(L1_gnn_conv_b)[:, :, 0],
        "w_x": by_halves(L1_gnn_w_xp),
        "w_dt": L1_gnn_w_dt,
        "b_dt": by_halves(L1_gnn_b_dt)[:, :, 0],
        "a_log": by_halves(L1_gnn_A_log),
        "d_skip": by_halves(L1_gnn_D_skip)[:, :, 0],
        "w_out": by_halves(L1_gnn_w_out),
        "ident_in": np.eye(P, dtype=np.float32),
    }
    nc = bacc.Bacc("TRN2", target_bir_lowering=False, num_devices=1)
    arrays, args = {}, {}
    for name, a in laid_out.items():
        arrays[name] = np.ascontiguousarray(a)
        args[name] = nc.dram_tensor(name, arrays[name].shape, F32, kind="ExternalInput").ap()
    out = nc.dram_tensor("out", (P, N), F32, kind="ExternalOutput").ap()
    build(nc, out=out, **args)
    got = run_bass_kernel_spmd(nc, [arrays], core_ids=[0]).results[0]["out"]
    return np.ascontiguousarray(got.reshape(P, N // P, F).transpose(1, 0, 2).reshape(N, F))
```
